# Optimizing a Trainium2 kernel written in Bass

```python
import numpy as np
import jax
import jax.numpy as jnp

def _softmax(x, axis=-1):
    return jax.nn.softmax(x, axis=axis)

def _gelu(x):
    return jax.nn.gelu(x, approximate=True)

def _silu(x):
    return jax.nn.silu(x)

def _sigmoid(x):
    return jax.nn.sigmoid(x)

def _layernorm(x, axis=-1, eps=1e-05):
    m = jnp.mean(x, axis=axis, keepdims=True)
    v = jnp.var(x, axis=axis, keepdims=True)
    return (x - m) / jnp.sqrt(v + eps)

def _scatter_add(tgt, idx, src, axis=0):
    return tgt.at[idx].add(src)

def _segment_sum(src, seg, n):
    return jax.ops.segment_sum(src, seg, n)
kernel_name = 'mk_hybrid_d1_jaxref_r8_05cb34'

def setup_inputs(seed: int=0):
    np.random.seed(seed)
    _w = jnp.asarray

    def _L0_attn_a_setup():
        import jax, jax.numpy as jnp
        import numpy as np
        BLOCK = 128

        def _block_cumsum_flat(x):
            shape = x.shape
            flat = x.reshape(-1, BLOCK)
            y = jnp.cumsum(flat, axis=-1)
            return y.reshape(shape)
        key = jax.random.key(seed)
        k1, k2, k3 = jax.random.split(key, 3)
        b, s, h = (8, 512, 128)
        x = jax.random.normal(k1, (b, s, h), dtype=jnp.float32)
        bound = 1.0 / np.sqrt(h)
        W = jax.random.uniform(k2, (h, h), dtype=jnp.float32, minval=-bound, maxval=bound)
        bias = jax.random.uniform(k3, (h,), dtype=jnp.float32, minval=-bound, maxval=bound)
        return {'x': x, 'W': W, 'bias': bias}
    _L0_attn_a_in = _L0_attn_a_setup()

    def _L0_attn_b_setup():
        import jax, jax.numpy as jnp
        import numpy as np
        D_MODEL = 128
        N_HEADS = 16
        D_K = D_MODEL // N_HEADS
        SEQ = 512
        BATCH = 2
        LOCAL_WINDOW = 128
        SCALE = 1.0 / float(np.sqrt(D_K))
        INIT = 1.0 / float(np.sqrt(D_MODEL))

        def _local_mask(seq_len: int) -> jnp.ndarray:
            i = jnp.arange(seq_len)[:, None]
            j = jnp.arange(seq_len)[None, :]
            return (j <= i) & (j >= i - LOCAL_WINDOW)
        key = jax.random.key(seed)
        ks = jax.random.split(key, 9)
        mk = lambda k: jax.random.normal(k, (D_MODEL, D_MODEL), dtype=jnp.float32) * INIT
        return {'x': jax.random.normal(ks[0], (BATCH, SEQ, D_MODEL), dtype=jnp.float32), 'Wq': mk(ks[1]), 'bq': jnp.zeros((D_MODEL,), jnp.float32), 'Wk': mk(ks[2]), 'bk': jnp.zeros((D_MODEL,), jnp.float32), 'Wv': mk(ks[3]), 'bv': jnp.zeros((D_MODEL,), jnp.float32), 'Wo': mk(ks[4]), 'bo': jnp.zeros((D_MODEL,), jnp.float32)}
    _L0_attn_b_in = _L0_attn_b_setup()

    def _L0_ffn_setup():
        import jax, jax.numpy as jnp
        import numpy as np
        E = 8
        K = 2
        D = 128
        H = 4 * D
        EPS = 1e-05
        TEMP = 1.5
        key = jax.random.key(seed)
        ks = jax.random.split(key, 6)
        B, T = (2, 256)
        x = jax.random.normal(ks[0], (B, T, D), dtype=jnp.float32)
        gamma = jnp.ones((D,), dtype=jnp.float32)
        beta = jnp.zeros((D,), dtype=jnp.float32)
        router_w = jax.random.normal(ks[1], (E, D), dtype=jnp.float32) * 0.02
        W1 = jax.random.normal(ks[2], (E, D, H), dtype=jnp.float32) * 0.02
        W2 = jax.random.normal(ks[3], (E, H, D), dtype=jnp.float32) * 0.02
        return {'x': x, 'gamma': gamma, 'beta': beta, 'router_w': router_w, 'W1': W1, 'W2': W2}
    _L0_ffn_in = _L0_ffn_setup()
    _d = {'L0_attn_a_x': _L0_attn_a_in['x'], 'L0_attn_a_W': _L0_attn_a_in['W'], 'L0_attn_a_bias': _L0_attn_a_in['bias'], 'L0_attn_b_Wq': _L0_attn_b_in['Wq'], 'L0_attn_b_bq': _L0_attn_b_in['bq'], 'L0_attn_b_Wk': _L0_attn_b_in['Wk'], 'L0_attn_b_bk': _L0_attn_b_in['bk'], 'L0_attn_b_Wv': _L0_attn_b_in['Wv'], 'L0_attn_b_bv': _L0_attn_b_in['bv'], 'L0_attn_b_Wo': _L0_attn_b_in['Wo'], 'L0_attn_b_bo': _L0_attn_b_in['bo'], 'L0_ffn_gamma': _L0_ffn_in['gamma'], 'L0_ffn_beta': _L0_ffn_in['beta'], 'L0_ffn_router_w': _L0_ffn_in['router_w'], 'L0_ffn_W1': _L0_ffn_in['W1'], 'L0_ffn_W2': _L0_ffn_in['W2']}
    _x0 = _d['L0_attn_a_x']
    _d['L0_attn_a_x'] = jax.random.normal(jax.random.fold_in(jax.random.key(seed), 1), (8, 512, 128), dtype=_x0.dtype)
    del _x0
    return _d

def reference(L0_attn_a_x, L0_attn_a_W, L0_attn_a_bias, L0_attn_b_Wq, L0_attn_b_bq, L0_attn_b_Wk, L0_attn_b_bk, L0_attn_b_Wv, L0_attn_b_bv, L0_attn_b_Wo, L0_attn_b_bo, L0_ffn_gamma, L0_ffn_beta, L0_ffn_router_w, L0_ffn_W1, L0_ffn_W2):

    def _L0_attn_a_ref(x, W, bias):
        import jax, jax.numpy as jnp
        import numpy as np
        BLOCK = 128

        def _block_cumsum_flat(x):
            shape = x.shape
            flat = x.reshape(-1, BLOCK)
            y = jnp.cumsum(flat, axis=-1)
            return y.reshape(shape)
        h = jnp.einsum('bsh,oh->bso', x, W) + bias
        return _block_cumsum_flat(h)

    def _L0_attn_b_ref(x, Wq, bq, Wk, bk, Wv, bv, Wo, bo):
        import jax, jax.numpy as jnp
        import numpy as np
        D_MODEL = 128
        N_HEADS = 16
        D_K = D_MODEL // N_HEADS
        SEQ = 512
        BATCH = 2
        LOCAL_WINDOW = 128
        SCALE = 1.0 / float(np.sqrt(D_K))
        INIT = 1.0 / float(np.sqrt(D_MODEL))

        def _local_mask(seq_len: int) -> jnp.ndarray:
            i = jnp.arange(seq_len)[:, None]
            j = jnp.arange(seq_len)[None, :]
            return (j <= i) & (j >= i - LOCAL_WINDOW)
        B, S, _ = x.shape
        q = (x @ Wq.T + bq).reshape(B, S, N_HEADS, D_K)
        k = (x @ Wk.T + bk).reshape(B, S, N_HEADS, D_K)
        v = (x @ Wv.T + bv).reshape(B, S, N_HEADS, D_K)
        scores = jnp.einsum('bqhd,bkhd->bhqk', q, k) * SCALE
        mask = _local_mask(S)[None, None]
        scores = jnp.where(mask, scores, jnp.float32(-10000.0))
        attn = jax.nn.softmax(scores, axis=-1) + jnp.float32(1e-09)
        ctx = jnp.einsum('bhqk,bkhd->bqhd', attn, v).reshape(B, S, D_MODEL)
        return ctx @ Wo.T + bo

    def _L0_ffn_ref(x, gamma, beta, router_w, W1, W2):
        import jax, jax.numpy as jnp
        import numpy as np
        E = 8
        K = 2
        D = 128
        H = 4 * D
        EPS = 1e-05
        TEMP = 1.5
        res = x
        mu = jnp.mean(x, axis=-1, keepdims=True)
        var = jnp.mean(jnp.square(x - mu), axis=-1, keepdims=True)
        xn = (x - mu) * jax.lax.rsqrt(var + EPS) * gamma + beta
        logits = jnp.einsum('btd,ed->bte', xn, router_w)
        probs = jax.nn.softmax(logits / TEMP, axis=-1)
        w, idx = jax.lax.top_k(probs, K)
        wdense = jnp.sum(jax.nn.one_hot(idx, E, dtype=w.dtype) * w[..., None], axis=-2)
        h = jax.nn.silu(jnp.einsum('btd,edf->betf', xn, W1))
        y = jnp.einsum('betf,efd->betd', h, W2)
        out = jnp.einsum('bte,betd->btd', wdense, y)
        return out + res
    x = L0_attn_a_x
    x = x + _L0_attn_a_ref(_layernorm(x, axis=-1), L0_attn_a_W, L0_attn_a_bias)
    x = x + _L0_ffn_ref(_layernorm(x, axis=-1), L0_ffn_gamma, L0_ffn_beta, L0_ffn_router_w, L0_ffn_W1, L0_ffn_W2)
    x = x + _L0_attn_b_ref(_layernorm(x, axis=-1), L0_attn_b_Wq, L0_attn_b_bq, L0_attn_b_Wk, L0_attn_b_bk, L0_attn_b_Wv, L0_attn_b_bv, L0_attn_b_Wo, L0_attn_b_bo)
    x = x + _L0_ffn_ref(_layernorm(x, axis=-1), L0_ffn_gamma, L0_ffn_beta, L0_ffn_router_w, L0_ffn_W1, L0_ffn_W2)
    return x

_drawn_inputs = setup_inputs


def setup_inputs(seed=0):
    import zlib

    import numpy as np

    out = dict(_drawn_inputs(seed))
    spreads = {'L0_attn_b_bq': (0.0, 0.8),
     'L0_attn_b_bk': (0.0, 0.8),
     'L0_attn_b_bv': (0.0, 0.354),
     'L0_attn_b_bo': (0.0, 0.354),
     'L0_ffn_gamma': (1.0, 0.6),
     'L0_ffn_beta': (0.0, 0.8)}
    factors = {'L0_ffn_router_w': 8.0, 'L0_ffn_W1': 8.0, 'L0_ffn_W2': 8.0}
    for name, (base, spread) in spreads.items():
        noise = np.random.default_rng([zlib.crc32(name.encode()), seed]).standard_normal(out[name].shape)
        drawn = base * np.exp(spread * noise) if base else spread * noise
        out[name] = jnp.asarray(drawn.astype(out[name].dtype))
    for name, factor in factors.items():
        out[name] = (out[name] * factor).astype(out[name].dtype)
    return out
```

```python
from contextlib import ExitStack

import concourse.bass as bass
from concourse import mybir

F32 = mybir.dt.float32
F16 = mybir.dt.float16
ALU = mybir.AluOpType
ACT = mybir.ActivationFunctionType
AX = mybir.AxisListType

P = 128
D = 128
B = 8
SEQ = 512
TPB = SEQ // P
NT = B * TPB
E = 8
H = 4 * D
FC = H // P
NH = 16
DK = D // NH
SETS = 4
EPS = 1e-5
TEMP = 1.5
SCALE = 1.0 / float(DK) ** 0.5
MASKED = -60000.0
ATTN_EPS = 1e-9
VW = DK + 1
VROW = NH * VW + 32
UNITS = SETS * TPB


def build(nc, x, wa, ba, wq, wk, wv, wo, bq, bk, bv, bo, gamma, beta, rw, w1, w2, out):
    x_t = x.rearrange("b (t p) d -> p (b t) d", p=P)
    out_t = out.rearrange("b (t p) d -> p (b t) d", p=P)
    dumps = nc.dram_tensor("dumps", [2, 4, P, SEQ], F16).ap()
    mdump = nc.dram_tensor("mdump", [2, NH, SEQ], F16).ap()

    with ExitStack() as ctx:
        def sb(n, s, d=F32):
            return ctx.enter_context(nc.sbuf_tensor(n, s, d))

        def ps(n, s, d=F32):
            return ctx.enter_context(nc.psum_tensor(n, s, d))

        def sem(n):
            return ctx.enter_context(nc.semaphore(n))

        def wait(eng, s, v):
            if not isinstance(v, int) or v > 0:
                eng.wait_ge(s, v)

        xs = sb("xs", [P, NT, D])
        wa_s = sb("wa_s", [P, D]); wc = sb("wc", [P, D]); cb = sb("cb", [1, D]); ba_s = sb("ba_s", [P, 1])
        wq_s = sb("wq_s", [P, D]); wk_s = sb("wk_s", [P, D]); wv_s = sb("wv_s", [P, D]); wo_s = sb("wo_s", [P, D])
        bq_s = sb("bq_s", [P, 1]); bk_s = sb("bk_s", [P, 1]); bv_s = sb("bv_s", [1, D]); bo_s = sb("bo_s", [1, D])
        ga_s = sb("ga_s", [P, 1]); be_s = sb("be_s", [P, 1]); rw_s = sb("rw_s", [P, E])
        w1_s = sb("w1_s", [P, E, H]); w2_s = sb("w2_s", [P, E, FC, D])
        ident = sb("ident", [P, P]); ident16 = sb("ident16", [P, P], F16)
        tri = sb("tri", [P, P]); ones_row = sb("ones_row", [1, P]); ones_col = sb("ones_col", [P, 1])
        esel = sb("esel", [E, E, P]); rank = sb("rank", [P, TPB, E])
        mband = sb("mband", [P, 2, 256], F16); mupper = sb("mupper", [P, 4, P], F16); mlower = sb("mlower", [P, 4, P], F16)
        mhalf = sb("mhalf", [P, 2, TPB])
        st = sb("st", [P, TPB, 6]); lsum = sb("lsum", [P, TPB]); ldif = sb("ldif", [P, TPB]); lm2 = sb("lm2", [P, TPB])
        lvar = sb("lvar", [P, TPB]); mean = sb("mean", [P, TPB]); ve = sb("ve", [P, 2, TPB]); r0 = sb("r0", [P, 2, TPB])
        nt_ = sb("nt_", [P, 2, TPB]); rr = sb("rr", [P, 2, TPB]); ubuf = sb("ubuf", [P, TPB, D])
        zr = sb("zr", [P, 2, TPB, D]); zT = sb("zT", [P, 2, SEQ])
        lg = sb("lg", [P, TPB, E]); pr = sb("pr", [P, TPB, E]); key = sb("key", [P, TPB, E]); oh1 = sb("oh1", [P, TPB, E])
        oh2 = sb("oh2", [P, TPB, E]); lg2 = sb("lg2", [P, TPB, E]); wd = sb("wd", [P, TPB, E])
        rm = sb("rm", [P, 4, TPB]); wT = sb("wT", [E, SEQ]); wB = sb("wB", [P, 2, SEQ])
        tanh = sb("tanh", [P, 2, SEQ]); hT = sb("hT", [P, 2, SEQ]); ytmp = sb("ytmp", [P, SEQ]); yacc = sb("yacc", [P, SEQ])
        hi = sb("hi", [P, 2, SEQ], F16); lo = sb("lo", [P, 2, SEQ], F16)
        qz = sb("qz", [P, 2, NH, SEQ], F16); kst = sb("kst", [P, 2, SETS, SEQ], F16)
        vp = sb("vp", [P, 2, TPB, VROW]); vsum = sb("vsum", [P, 2, 1]); vrow = sb("vrow", [1, D])
        mx = sb("mx", [P, TPB, NH], F16); mT = sb("mT", [NH, SEQ], F16)
        pT = sb("pT", [P, 2, 4, 256]); uT = sb("uT", [P, SETS, SEQ]); cx = sb("cx", [P, TPB, D]); rden = sb("rden", [P, TPB, NH])
        cT = sb("cT", [P, SEQ])

        bank = [ps(f"bank{i}", [P, 512]) for i in range(2)]
        sbank = ps("sbank", [P, 2, 512])
        stbank = ps("stbank", [P, 4, 512])

        s_x = [sem(f"x{b}_loaded") for b in range(B)]; s_w = sem("weights_loaded"); s_wff = sem("ffn_weights_loaded")
        s_const = sem("constants_made"); s_chain = sem("pool_chain"); s_wcp = sem("wc_psum"); s_wcs = sem("wc_ready")
        s_ve = sem("variance_ready"); s_r0 = sem("rsqrt_guess")
        s_z = sem("z_ready"); s_zp = sem("z_transposed"); s_zt = sem("zt_ready"); s_ztf = sem("zt_used")
        s_am = sem("linear_psum"); s_aa = sem("linear_added")
        s_lg = sem("logits_psum"); s_lc = sem("logits_centred"); s_pe = sem("probs_exp"); s_wd = sem("wdense_ready")
        s_wtp = sem("wt_psum"); s_wt = sem("wt_ready"); s_wbp = sem("wb_psum"); s_wb = sem("wb_ready")
        s_h = sem("h_psum"); s_th = sem("tanh_ready"); s_ht = sem("ht_ready"); s_hu = sem("ht_used")
        s_y = sem("y_psum"); s_yt = sem("y_taken"); s_ytp = sem("y_transposed"); s_ya = sem("y_added")
        s_qk = sem("qk_psum"); s_hi = sem("hi_ready"); s_lo = sem("lo_ready"); s_vm = sem("v_psum"); s_v = sem("v_ready")
        s_vs = sem("vsum_psum"); s_vsr = sem("vsum_ready")
        s_dump = sem("qk_dumped"); s_stk = sem("stacks_loaded")
        s_s = sem("s_psum"); s_red = sem("s_reduced"); s_mtp = sem("max_transposed"); s_mt = sem("max_ready")
        s_md = sem("max_dumped"); s_mr = sem("max_row_loaded")
        s_st = sem("st_psum"); s_e = sem("exp_ready"); s_pv = sem("pv_done"); s_u = sem("u_copied")
        s_ut = sem("u_transposed"); s_cx = sem("ctx_ready"); s_cxp = sem("ctx_transposed"); s_ct = sem("ct_ready")
        s_o = sem("o_psum"); s_oa = sem("o_added"); s_out = sem("stored")

        block = ctx.enter_context(nc.Block())
        N_W, N_CONST = 13, 12
        LAST_ADD = 2 * B

        @block.sync
        def _(sp):
            for b in range(B):
                sp.dma_start(xs[:, TPB * b:TPB * b + TPB, :], x_t[:, TPB * b:TPB * b + TPB, :]).then_inc(s_x[b], 16)
            for d, s in ((wa_s, wa), (ba_s, ba), (wq_s, wq), (wk_s, wk), (wv_s, wv), (wo_s, wo), (bq_s, bq), (bk_s, bk),
                         (bv_s, bv), (bo_s, bo), (ga_s, gamma), (be_s, beta), (rw_s, rw)):
                sp.dma_start(d[:], s).then_inc(s_w, 16)
            sp.dma_start(w1_s[:], w1.rearrange("e d f -> d e f")).then_inc(s_wff, 16)
            sp.dma_start(w2_s[:], w2.rearrange("e (c p) d -> p e c d", p=P)).then_inc(s_wff, 16)
            for b in range(B):
                par = b % 2
                for i in range(2):
                    sp.wait_ge(s_hi, 2 * b + i + 1)
                    sp.dma_start(dumps[par, 2 * i], hi[:, i, :]).then_inc(s_dump, 16)
                    sp.wait_ge(s_lo, 2 * b + i + 1)
                    sp.dma_start(dumps[par, 2 * i + 1], lo[:, i, :]).then_inc(s_dump, 16)
                sp.wait_ge(s_dump, 64 * (b + 1))
                wait(sp, s_pv, UNITS * (b - 1))
                wait(sp, s_s, UNITS * (b - 1))
                for i, parts in ((0, (0, 0, 1)), (1, (0, 1, 0))):
                    for g in range(4):
                        for c in range(3):
                            src = dumps[par, 2 * i + parts[c]].rearrange("(g s j) n -> g j s n", g=4, s=SETS)[g]
                            r = 32 * g + DK * c
                            dst = (qz[r:r + DK, par, g * SETS:(g + 1) * SETS, :] if i == 0 else kst[r:r + DK, par, :, :])
                            sp.dma_start(dst, src).then_inc(s_stk, 16)
                sp.wait_ge(s_mt, b + 1)
                sp.dma_start(mdump[par], mT[:]).then_inc(s_md, 16)
                sp.wait_ge(s_md, 16 * (b + 1))
                sp.dma_start(qz[P - 1:P, par, :, :], mdump[par].rearrange("(a h) n -> a h n", a=1)).then_inc(s_mr, 16)
            for b in range(B):
                sp.wait_ge(s_ya, B + b + 1)
                sp.dma_start(out_t[:, TPB * b:TPB * b + TPB, :], xs[:, TPB * b:TPB * b + TPB, :]).then_inc(s_out, 16)
            sp.wait_ge(s_out, 16 * B)

        @block.gpsimd
        def _(pool):
            g = nc.gpsimd
            n = 0
            for t, v in ((ident, 0.0), (tri, 1.0), (ones_row, 1.0), (ones_col, 1.0), (esel, 0.0), (mband, 0.0),
                         (mupper, 0.0), (mlower, 0.0), (mhalf, -0.5), (vp, 1.0), (kst, 0.0)):
                g.memset(t[:], v).then_inc(s_chain, 1)
                n += 1
            g.memset(qz[:].bitcast(F32), 0.0).then_inc(s_chain, 1)
            for e in range(E):
                g.memset(rank[:, :, e], float(E - e)).then_inc(s_chain, 1)
            pool.wait_ge(s_chain, n + 1 + E)
            n += 1 + E
            g.affine_select(out=ident[:], in_=ident[:], compare_op=ALU.not_equal, fill=1.0, base=0,
                            pattern=[[1, P]], channel_multiplier=-1).then_inc(s_chain, 1)
            g.affine_select(out=tri[:], in_=tri[:], compare_op=ALU.is_ge, fill=0.0, base=0,
                            pattern=[[1, P]], channel_multiplier=-1).then_inc(s_const, 1)
            g.affine_select(out=esel[:], in_=esel[:], compare_op=ALU.not_equal, fill=1.0, base=0,
                            pattern=[[1, E], [0, P]], channel_multiplier=-1).then_inc(s_const, 1)
            g.affine_select(out=mband[:], in_=mband[:], compare_op=ALU.is_ge, fill=MASKED, base=0,
                            pattern=[[0, 2], [1, 256]], channel_multiplier=-1).then_inc(s_chain, 1)
            g.affine_select(out=mupper[:], in_=mupper[:], compare_op=ALU.is_ge, fill=MASKED, base=0,
                            pattern=[[0, 4], [1, P]], channel_multiplier=-1).then_inc(s_const, 1)
            g.affine_select(out=mlower[:], in_=mlower[:], compare_op=ALU.is_ge, fill=MASKED, base=0,
                            pattern=[[0, 4], [-1, P]], channel_multiplier=1).then_inc(s_const, 1)
            g.affine_select(out=kst[:], in_=kst[:], compare_op=ALU.not_equal, fill=1.0, base=-(P - 1),
                            pattern=[[0, 2], [0, SETS], [0, SEQ]], channel_multiplier=1).then_inc(s_const, 1)
            pool.wait_ge(s_chain, n + 2)
            g.affine_select(out=mband[:], in_=mband[:], compare_op=ALU.is_ge, fill=MASKED, base=P,
                            pattern=[[0, 2], [-1, 256]], channel_multiplier=1).then_inc(s_const, 1)
            g.tensor_copy(ident16[:], ident[:]).then_inc(s_const, 7)
            for i in range(4 * B):
                pool.wait_ge(s_ve, i + 1)
                g.tensor_tensor(r0[:], ve[:], mhalf[:], ALU.pow).then_inc(s_r0, 1)

        @block.vector
        def _(dve):
            v = nc.vector

            def norm_stats(n, b):
                for t in range(TPB):
                    v.bn_stats(st[:, t, :], xs[:, TPB * b + t, :])
                dve.drain()
                v.tensor_tensor(lsum[:], st[:, :, 1], st[:, :, 4], ALU.add)
                v.tensor_tensor(ldif[:], st[:, :, 1], st[:, :, 4], ALU.subtract)
                v.tensor_tensor(lm2[:], st[:, :, 2], st[:, :, 5], ALU.add)
                dve.drain()
                v.tensor_scalar(mean[:], lsum[:], 0.5, None, ALU.mult)
                v.tensor_tensor(ldif[:], ldif[:], ldif[:], ALU.mult)
                v.tensor_scalar(lm2[:], lm2[:], 1.0 / D, None, ALU.mult)
                dve.drain()
                v.scalar_tensor_tensor(out=lvar[:], in0=ldif[:], scalar=0.25, in1=lm2[:], op0=ALU.mult, op1=ALU.add)
                dve.drain()
                v.tensor_scalar(ve[:, 0, :], lvar[:], EPS, None, ALU.add)
                v.tensor_scalar(ve[:, 1, :], lvar[:], 1.0 + EPS, EPS * EPS, ALU.mult, ALU.add).then_inc(s_ve, 1)
                dve.wait_ge(s_r0, n + 1)
                v.tensor_tensor(nt_[:], r0[:], r0[:], ALU.mult)
                dve.drain()
                v.tensor_tensor(nt_[:], nt_[:], ve[:], ALU.mult)
                dve.drain()
                v.tensor_scalar(nt_[:], nt_[:], -0.5, 1.5, ALU.mult, ALU.add)
                dve.drain()
                v.tensor_tensor(rr[:], r0[:], nt_[:], ALU.mult)
                dve.drain()

            def normalise(n, b, which):
                par = b % 2
                wait(dve, s_zp, n - 1)
                for t in range(TPB):
                    ins = v.tensor_scalar(zr[:, par, t, :], xs[:, TPB * b + t, :], mean[:, t:t + 1],
                                          rr[:, which, t:t + 1], ALU.subtract, ALU.mult)
                ins.then_inc(s_z, 1)

            def stage_a(b):
                dve.wait_ge(s_x[b], 16)
                norm_stats(b, b)
                normalise(b, b, 0)

            def stage_a_add(b):
                dve.wait_ge(s_am, b + 1)
                xb = xs[:, TPB * b:TPB * b + TPB, :].rearrange("p t d -> p (t d)")
                v.tensor_tensor(xb, xb, sbank[:, b % 2, :], ALU.add).then_inc(s_aa, 1)

            def route(m):
                def bc(a):
                    return a.unsqueeze(2).to_broadcast([P, TPB, E])
                dve.wait_ge(s_lg, m + 1)
                v.tensor_copy(lg[:], bank[1][:, 0:TPB * E].rearrange("p (t e) -> p t e", e=E))
                dve.drain()
                v.tensor_reduce(rm[:, 0, :], lg[:], AX.X, ALU.max)
                dve.drain()
                v.tensor_tensor(lg[:], lg[:], bc(rm[:, 0, :]), ALU.subtract).then_inc(s_lc, 1)
                dve.drain()
                v.scalar_tensor_tensor(out=key[:], in0=lg[:], scalar=0.0, in1=rank[:], op0=ALU.is_equal, op1=ALU.mult)
                dve.drain()
                v.tensor_reduce(rm[:, 1, :], key[:], AX.X, ALU.max)
                dve.drain()
                v.tensor_tensor(oh1[:], key[:], bc(rm[:, 1, :]), ALU.is_equal)
                dve.drain()
                v.scalar_tensor_tensor(out=lg2[:], in0=oh1[:], scalar=-1e30, in1=lg[:], op0=ALU.mult, op1=ALU.add)
                dve.drain()
                v.tensor_reduce(rm[:, 2, :], lg2[:], AX.X, ALU.max)
                dve.drain()
                v.tensor_tensor(key[:], lg2[:], bc(rm[:, 2, :]), ALU.is_equal)
                dve.drain()
                v.tensor_tensor(key[:], key[:], rank[:], ALU.mult)
                dve.drain()
                v.tensor_reduce(rm[:, 1, :], key[:], AX.X, ALU.max)
                dve.drain()
                v.tensor_tensor(oh2[:], key[:], bc(rm[:, 1, :]), ALU.is_equal)
                dve.drain()
                v.tensor_tensor(oh1[:], oh1[:], oh2[:], ALU.add)
                dve.wait_ge(s_pe, m + 1)
                v.tensor_reduce(rm[:, 3, :], pr[:], AX.X, ALU.add)
                dve.drain()
                v.reciprocal(rm[:, 3, :], rm[:, 3, :])
                v.tensor_tensor(oh1[:], oh1[:], pr[:], ALU.mult)
                dve.drain()
                v.tensor_tensor(wd[:], oh1[:], bc(rm[:, 3, :]), ALU.mult).then_inc(s_wd, 1)

            def ffn(layer, b):
                n = B * (1 + 2 * layer) + b
                m = B * layer + b
                xb = xs[:, TPB * b:TPB * b + TPB, :].rearrange("p t d -> p (t d)")
                norm_stats(n, b)
                normalise(n, b, 1)
                for t in range(TPB):
                    v.tensor_scalar(ubuf[:, t, :], xs[:, TPB * b + t, :], mean[:, t:t + 1], rr[:, 0, t:t + 1],
                                    ALU.subtract, ALU.mult)
                dve.drain()
                v.tensor_tensor(xb, xb, ubuf[:].rearrange("p t d -> p (t d)"), ALU.add)
                route(m)
                for e in range(E):
                    for f in range(FC):
                        i = (m * E + e) * FC + f
                        dve.wait_ge(s_th, i + 1)
                        wait(dve, s_hu, i - 1)
                        v.scalar_tensor_tensor(out=hT[:, i % 2, :], in0=tanh[:, i % 2, :], scalar=1.0,
                                               in1=stbank[:, i % 2, :], op0=ALU.add, op1=ALU.mult).then_inc(s_ht, 1)
                    k = m * E + e
                    dve.wait_ge(s_y, k + 1)
                    dve.wait_ge(s_wb, k + 1)
                    dst = yacc if e == 0 else ytmp
                    ins = v.tensor_tensor(dst[:], stbank[:, 2 + k % 2, :], wB[:, k % 2, :], ALU.mult)
                    ins.then_inc(s_yt, 1)
                    if e:
                        dve.drain()
                        v.tensor_tensor(yacc[:], yacc[:], ytmp[:], ALU.add)
                    dve.drain()
                v.tensor_copy(ytmp[:], yacc[:]).then_inc(s_yt, 1)
                dve.wait_ge(s_ytp, m + 1)
                v.tensor_tensor(xb, xb, sbank[:, 0, :], ALU.add).then_inc(s_ya, 1)
                dve.drain()

            for b in range(B):
                stage_a(b)
                if b:
                    stage_a_add(b - 1)
            stage_a_add(B - 1)
            dve.drain()
            for b in range(B):
                ffn(0, b)

            def front(b):
                norm_stats(2 * B + b, b)
                normalise(2 * B + b, b, 0)
                for i, bias in ((0, bq_s), (1, bk_s)):
                    dve.wait_ge(s_hi, 2 * b + i + 1)
                    wait(dve, s_dump, 64 * b)
                    v.scalar_tensor_tensor(out=lo[:, i, :], in0=sbank[:, i, :], scalar=bias[:, 0:1], in1=hi[:, i, :],
                                           op0=ALU.add, op1=ALU.subtract).then_inc(s_lo, 1)

            def reduce(b, j):
                s, qt = j // TPB, j % TPB
                dve.wait_ge(s_s, UNITS * b + j + 1)
                w = 256 if qt else 128
                src = sbank[:].rearrange("p a n -> p (a n)")[:, 0:4 * w].rearrange("p (h k) -> p h k", k=w)
                if j == 0:
                    wait(dve, s_mtp, b)
                v.tensor_reduce(mx[:, qt, 4 * s:4 * s + 4], src, AX.X, ALU.max, negate=True).then_inc(s_red, 1)

            def back(b):
                for qt in range(TPB):
                    dve.wait_ge(s_ut, TPB * b + qt + 1)
                    u = sbank[:, qt % 2, :].rearrange("p (h r) -> p h r", r=32)
                    v.reciprocal(rden[:, qt, :], u[:, :, DK])
                    dve.drain()
                    v.tensor_tensor(cx[:, qt, :].rearrange("p (h j) -> p h j", j=DK), u[:, :, 0:DK],
                                    rden[:, qt, :].unsqueeze(2).to_broadcast([P, NH, DK]), ALU.mult).then_inc(s_cx, 1)
                dve.wait_ge(s_o, b + 1)
                xb = xs[:, TPB * b:TPB * b + TPB, :].rearrange("p t d -> p (t d)")
                v.tensor_tensor(xb, xb, bank[1][:, :], ALU.add).then_inc(s_oa, 1)

            for b in range(B):
                front(b)
                for j in range(UNITS):
                    reduce(b, j)
                back(b)
            dve.drain()
            for b in range(B):
                ffn(1, b)

        @block.scalar
        def _(act):
            a = nc.scalar

            def evac_z(n, scale=None):
                act.wait_ge(s_zp, n + 1)
                wait(act, s_ztf, n - 1)
                if scale is None:
                    a.activation(zT[:, n % 2, :], bank[0][:, :], ACT.Copy).then_inc(s_zt, 1)
                else:
                    a.activation(zT[:, n % 2, :], bank[0][:, :], ACT.Identity, scale=ga_s[:, 0:1],
                                 bias=be_s[:, 0:1]).then_inc(s_zt, 1)

            act.wait_ge(s_w, 16 * N_W)
            act.wait_ge(s_wcp, 1)
            a.activation(wc[:], bank[0][:, 0:D], ACT.Copy).then_inc(s_wcs, 1)
            a.activation(cb[:], bank[0][0:1, D:2 * D], ACT.Copy).then_inc(s_wcs, 1)
            for b in range(B):
                evac_z(b)

            def ffn(layer, b):
                n = B * (1 + 2 * layer) + b
                m = B * layer + b
                evac_z(n, True)
                act.wait_ge(s_lc, m + 1)
                a.activation(pr[:], lg[:], ACT.Exp, scale=1.0 / TEMP).then_inc(s_pe, 1)
                act.wait_ge(s_wtp, m + 1)
                a.activation(wT[:], bank[1][0:E, :], ACT.Copy, scale=0.5).then_inc(s_wt, 1)
                for e in range(E):
                    k = m * E + e
                    act.wait_ge(s_wbp, k + 1)
                    wait(act, s_yt, (E + 1) * m + e - 1)
                    a.activation(wB[:, k % 2, :], bank[1][:, :], ACT.Copy).then_inc(s_wb, 1)
                    for f in range(FC):
                        i = k * FC + f
                        act.wait_ge(s_h, i + 1)
                        wait(act, s_ht, i - 1)
                        a.activation(tanh[:, i % 2, :], stbank[:, i % 2, :], ACT.Tanh, scale=0.5).then_inc(s_th, 1)

            for b in range(B):
                ffn(0, b)

            def front(b):
                par = b % 2
                evac_z(2 * B + b)
                for i, bias in ((0, bq_s), (1, bk_s)):
                    act.wait_ge(s_qk, 2 * b + i + 1)
                    wait(act, s_dump, 64 * b)
                    a.activation(hi[:, i, :], sbank[:, i, :], ACT.Identity, bias=bias[:, 0:1]).then_inc(s_hi, 1)
                act.wait_ge(s_vm, b + 1)
                wait(act, s_pv, UNITS * (b - 1))
                dst = vp[:, par, :, 0:NH * VW].rearrange("p t (h j) -> p t h j", j=VW)
                for t in range(TPB):
                    ins = a.activation(dst[:, t, :, 0:DK], bank[1][:, P * t:P * t + P].rearrange("p (h j) -> p h j", j=DK), ACT.Copy)
                ins.then_inc(s_v, 1)
                act.wait_ge(s_vs, 2 * b + 1)
                a.activation(vrow[:], bank[1][0:1, 0:D], ACT.Copy, scale=ATTN_EPS).then_inc(s_vsr, 1)
                act.wait_ge(s_vs, 2 * b + 2)
                a.activation(vsum[:, par, :], bank[1][:, 0:1], ACT.Copy).then_inc(s_vsr, 1)

            def exps(b, j):
                kt = j % TPB
                w = 256 if kt < TPB - 1 else 128
                i = UNITS * b + j
                act.wait_ge(s_st, i + 1)
                wait(act, s_pv, i - 1)
                src = stbank[:].rearrange("p a n -> p (a n)")[:, 1024 * (j % 2):1024 * (j % 2) + 4 * w]
                dst = pT[:].rearrange("p u h q -> p u (h q)")[:, j % 2, 0:4 * w]
                a.activation(dst, src, ACT.Exp, scale=SCALE).then_inc(s_e, 1)

            def u_copy(b, s):
                act.wait_ge(s_pv, UNITS * b + TPB * (s + 1))
                wait(act, s_ut, TPB * b)
                a.activation(uT[:, s, :], bank[0][:, :], ACT.Copy).then_inc(s_u, 1)

            for b in range(B):
                front(b)
                act.wait_ge(s_mtp, b + 1)
                wait(act, s_md, 16 * b)
                a.activation(mT[:], bank[1][0:NH, 0:SEQ // 2].bitcast(F16), ACT.Copy).then_inc(s_mt, 1)
                for j in range(UNITS):
                    exps(b, j)
                    if j and j % TPB == 0:
                        u_copy(b, j // TPB - 1)
                u_copy(b, SETS - 1)
                act.wait_ge(s_cxp, b + 1)
                a.activation(cT[:], bank[0][:, :], ACT.Identity, bias=vsum[:, b % 2, :]).then_inc(s_ct, 1)
            for b in range(B):
                ffn(1, b)

        @block.tensor
        def _(pe):
            mm = pe.matmul
            pe.wait_ge(s_const, N_CONST)
            pe.wait_ge(s_w, 16 * N_W)
            mm(bank[0][:, 0:D], wa_s[:], tri[:], start=True, stop=True)
            mm(bank[0][0:1, D:2 * D], ba_s[:], tri[:], start=True, stop=True).then_inc(s_wcp, 1)
            pe.wait_ge(s_wcs, 2)

            def transpose_z(n):
                pe.wait_ge(s_z, n + 1)
                for t in range(TPB):
                    ins = pe.transpose(bank[0][:, P * t:P * t + P], zr[:, n % 2, t, :], ident[:])
                ins.then_inc(s_zp, 1)
                pe.wait_ge(s_zt, n + 1)

            for b in range(B):
                transpose_z(b)
                wait(pe, s_aa, b - 1)
                for t in range(TPB):
                    o = sbank[:, b % 2, P * t:P * t + P]
                    mm(o, zT[:, b % 2, P * t:P * t + P], wc[:], start=True, stop=False)
                    ins = mm(o, ones_row[:], cb[:], start=False, stop=True)
                ins.then_inc(s_am, 1)
                pe.sem_inc(s_ztf, 1)

            pe.wait_ge(s_wff, 32)

            def ffn(layer, b):
                n = B * (1 + 2 * layer) + b
                m = B * layer + b
                if b == 0:
                    if layer == 0:
                        pe.wait_ge(s_aa, B)
                    else:
                        pe.wait_ge(s_oa, B)
                transpose_z(n)
                par = n % 2
                if m:
                    pe.wait_ge(s_wb, E * m)
                for t in range(TPB):
                    ins = mm(bank[1][:, E * t:E * t + E], zT[:, par, P * t:P * t + P], rw_s[:], start=True, stop=True)
                ins.then_inc(s_lg, 1)
                pe.wait_ge(s_wd, m + 1)
                for t in range(TPB):
                    ins = pe.transpose(bank[1][0:E, P * t:P * t + P], wd[:, t, :], ident[:])
                ins.then_inc(s_wtp, 1)
                pe.wait_ge(s_wt, m + 1)
                for e in range(E):
                    k = m * E + e
                    if e:
                        pe.wait_ge(s_wb, k)
                    mm(bank[1][:, :], esel[:, e, :], wT[:], start=True, stop=True).then_inc(s_wbp, 1)
                    for f in range(FC + 1):
                        i = k * FC + f
                        if f < FC:
                            wait(pe, s_ht, i - 1)
                            mm(stbank[:, i % 2, :], w1_s[:, e, P * f:P * f + P], zT[:, par, :], start=True,
                               stop=True).then_inc(s_h, 1)
                        if f:
                            if f == 1:
                                wait(pe, s_yt, (E + 1) * m + e - 1 if e > 1 else (E + 1) * m - 1 + e)
                            pe.wait_ge(s_ht, i)
                            mm(stbank[:, 2 + k % 2, :], w2_s[:, e, f - 1, :], hT[:, (i - 1) % 2, :], start=(f == 1),
                               stop=(f == FC)).then_inc(s_hu, 1)
                    pe.wait_ge(s_hu, (k + 1) * FC)
                    pe.sem_inc(s_y, 1)
                pe.sem_inc(s_ztf, 1)
                pe.wait_ge(s_yt, (E + 1) * (m + 1))
                for t in range(TPB):
                    ins = pe.transpose(sbank[:, 0, P * t:P * t + P], ytmp[:, P * t:P * t + P], ident[:])
                ins.then_inc(s_ytp, 1)
                if b < B - 1 or True:
                    pe.wait_ge(s_ya, m + 1)

            for b in range(B):
                ffn(0, b)

            def front(b):
                n = 2 * B + b
                par = b % 2
                transpose_z(n)
                wait(pe, s_red, UNITS * b)
                wait(pe, s_cx, TPB * b)
                for i, w in ((0, wq_s), (1, wk_s)):
                    mm(sbank[:, i, :], w[:], zT[:, par, :], start=True, stop=True).then_inc(s_qk, 1)
                for t in range(TPB):
                    o = bank[1][:, P * t:P * t + P]
                    mm(o, zT[:, par, P * t:P * t + P], wv_s[:], start=True, stop=False)
                    ins = mm(o, ones_row[:], bv_s[:], start=False, stop=True)
                ins.then_inc(s_vm, 1)
                pe.sem_inc(s_ztf, 1)
                pe.wait_ge(s_v, b + 1)
                for t in range(TPB):
                    vt = vp[:, par, t, 0:NH * VW].rearrange("p (h j) -> p h j", j=VW)[:, :, 0:DK]
                    ins = mm(bank[1][0:1, 0:D], ones_col[:], vt, start=(t == 0), stop=(t == TPB - 1))
                ins.then_inc(s_vs, 1)
                pe.wait_ge(s_vsr, 2 * b + 1)
                mm(bank[1][:, 0:1], vrow[:], ones_row[0:1, 0:1], start=True, stop=True).then_inc(s_vs, 1)
                pe.wait_ge(s_vsr, 2 * b + 2)

            def scores(b, j):
                s, qt = j // TPB, j % TPB
                par = b % 2
                wait(pe, s_red, UNITS * b + j)
                w = 256 if qt else 128
                flat = sbank[:].rearrange("p a n -> p (a n)")
                for a2 in range(2 if qt else 1):
                    mask = (mband[:].rearrange("p a n -> p (a n)") if qt else mlower[:].rearrange("p a n -> p (a n)"))
                    mm(flat[:, 512 * a2:512 * a2 + 512], ident16[:], mask, start=True, stop=False, skip_group_check=True)
                k0 = P * (qt - 1) if qt else 0
                for g in range(4):
                    ins = mm(flat[:, w * g:w * g + w], qz[0:P - 1, par, g * SETS + s, P * qt:P * qt + P],
                             kst[0:P - 1, par, s, k0:k0 + w], start=False, stop=True, skip_group_check=True)
                ins.then_inc(s_s, 1)

            def scores_t(b, j):
                s, kt = j // TPB, j % TPB
                par = b % 2
                wait(pe, s_e, UNITS * b + j - 1)
                w = 256 if kt < TPB - 1 else 128
                flat = stbank[:].rearrange("p a n -> p (a n)")[:, 1024 * (j % 2):1024 * (j % 2) + 1024]
                for a2 in range(2 if w == 256 else 1):
                    mask = (mband if w == 256 else mupper)[:].rearrange("p a n -> p (a n)")
                    mm(flat[:, 512 * a2:512 * a2 + 512], ident16[:], mask, start=True, stop=False, skip_group_check=True)
                for g in range(4):
                    ins = mm(flat[:, w * g:w * g + w], kst[:, par, s, P * kt:P * kt + P],
                             qz[:, par, g * SETS + s, P * kt:P * kt + w], start=False, stop=True, skip_group_check=True)
                ins.then_inc(s_st, 1)

            def pv(b, j):
                s, kt = j // TPB, j % TPB
                par = b % 2
                w = 256 if kt < TPB - 1 else 128
                pe.wait_ge(s_e, UNITS * b + j + 1)
                if kt == 0:
                    wait(pe, s_u, SETS * b + s)
                for g in range(4):
                    h = SETS * s + g
                    src = pT[:].rearrange("p u h q -> p u (h q)")[:, j % 2, w * g:w * g + w]
                    ins = mm(bank[0][32 * g:32 * g + 32, P * kt:P * kt + w], vp[:, par, kt, VW * h:VW * h + 32], src,
                             start=(kt == 0), stop=(kt == TPB - 1), tile_position=(0, 32 * g), skip_group_check=True)
                ins.then_inc(s_pv, 1)

            def back(b):
                pe.wait_ge(s_u, SETS * (b + 1))
                for qt in range(TPB):
                    if qt >= 2:
                        pe.wait_ge(s_cx, TPB * b + qt - 1)
                    for s in range(SETS):
                        ins = pe.transpose(sbank[:, qt % 2, P * s:P * s + P], uT[:, s, P * qt:P * qt + P], ident[:])
                    ins.then_inc(s_ut, 1)
                for qt in range(TPB):
                    pe.wait_ge(s_cx, TPB * b + qt + 1)
                    ins = pe.transpose(bank[0][:, P * qt:P * qt + P], cx[:, qt, :], ident[:])
                ins.then_inc(s_cxp, 1)
                pe.wait_ge(s_ct, b + 1)
                for t in range(TPB):
                    o = bank[1][:, P * t:P * t + P]
                    mm(o, cT[:, P * t:P * t + P], wo_s[:], start=True, stop=False)
                    ins = mm(o, ones_row[:], bo_s[:], start=False, stop=True)
                ins.then_inc(s_o, 1)
                pe.wait_ge(s_oa, b + 1)

            for b in range(B):
                front(b)
                pe.wait_ge(s_stk, 384 * (b + 1))
                pe.wait_ge(s_lo, 2 * (b + 1))
                for j in range(UNITS):
                    scores(b, j)
                pe.wait_ge(s_red, UNITS * (b + 1))
                for t in range(TPB):
                    ins = pe.transpose(bank[1][0:NH, P // 2 * t:P // 2 * t + P // 2].bitcast(F16), mx[:, t, :], ident16[:])
                ins.then_inc(s_mtp, 1)
                pe.wait_ge(s_mr, 16 * (b + 1))
                for j in range(UNITS + 1):
                    if j < UNITS:
                        scores_t(b, j)
                    if j:
                        pv(b, j - 1)
                back(b)
            for b in range(B):
                ffn(1, b)


def head_order():
    return [DK * (SETS * s + g) + j for g in range(4) for s in range(SETS) for j in range(DK)]


def kernel(L0_attn_a_x, L0_attn_a_W, L0_attn_a_bias, L0_attn_b_Wq, L0_attn_b_bq, L0_attn_b_Wk, L0_attn_b_bk,
           L0_attn_b_Wv, L0_attn_b_bv, L0_attn_b_Wo, L0_attn_b_bo, L0_ffn_gamma, L0_ffn_beta, L0_ffn_router_w,
           L0_ffn_W1, L0_ffn_W2):
    import numpy as np
    import concourse.bacc as bacc
    from concourse.bass_utils import run_bass_kernel_spmd

    order = head_order()
    layout = {
        "x": L0_attn_a_x, "wa": L0_attn_a_W, "ba": np.reshape(L0_attn_a_bias, (D, 1)),
        "wq": np.transpose(L0_attn_b_Wq)[:, order], "wk": np.transpose(L0_attn_b_Wk)[:, order],
        "wv": np.transpose(L0_attn_b_Wv), "wo": np.transpose(L0_attn_b_Wo),
        "bq": np.reshape(np.asarray(L0_attn_b_bq)[order], (D, 1)), "bk": np.reshape(np.asarray(L0_attn_b_bk)[order], (D, 1)),
        "bv": np.reshape(L0_attn_b_bv, (1, D)), "bo": np.reshape(L0_attn_b_bo, (1, D)),
        "gamma": np.reshape(L0_ffn_gamma, (D, 1)), "beta": np.reshape(L0_ffn_beta, (D, 1)),
        "rw": np.transpose(L0_ffn_router_w), "w1": L0_ffn_W1, "w2": L0_ffn_W2,
    }
    nc = bacc.Bacc("TRN2", target_bir_lowering=False, num_devices=1)
    arrays, args = {}, []
    for name, a in layout.items():
        a = np.ascontiguousarray(a)
        arrays[f"in_{name}"] = a
        args.append(nc.dram_tensor(f"in_{name}", a.shape, mybir.dt.from_np(a.dtype), kind="ExternalInput").ap())
    args.append(nc.dram_tensor("out", (B, SEQ, D), F32, kind="ExternalOutput").ap())
    build(nc, *args)
    r = run_bass_kernel_spmd(nc, [arrays], core_ids=[0])
    return r.results[0]["out"]
```

```python
from contextlib import ExitStack

import concourse.bass as bass
from concourse import mybir

F32 = mybir.dt.float32
F16 = mybir.dt.float16
I32 = mybir.dt.int32
U32 = mybir.dt.uint32
ALU = mybir.AluOpType
ACT = mybir.ActivationFunctionType
AX = mybir.AxisListType

P = 128
D = 128
B = 8
SEQ = 512
TPB = SEQ // P
NT = B * TPB
E = 8
H = 4 * D
FC = H // P
NH = 16
DK = D // NH
SETS = 4
EPS = 1e-5
TEMP = 1.5
SCALE = 1.0 / float(DK) ** 0.5
MASKED = -60000.0
ATTN_EPS = 1e-9
VW = DK + 1
VROW = NH * VW + 32
UNITS = SETS * TPB

BPC = 4
CT = BPC * TPB
CHUNK = CT * P
CHUNKS = B // BPC
SLOT_TILES = (2 * CHUNK + E * (P - 1)) // P
WSCALE = 64.0
G = 4
LOADS = 4
PIECES_A = 11
PIECES_R = 22


def build(nc, x, wa, ba, wq, wk, wv, wo, bq, bk, bv, bo, gamma, beta, rw, w1, w2, out):
    x_t = x.rearrange("b (t p) d -> p (b t) d", p=P)
    out_t = out.rearrange("b (t p) d -> p (b t) d", p=P)
    dumps = nc.dram_tensor("dumps", [2, 4, P, SEQ], F16).ap()
    mdump = nc.dram_tensor("mdump", [2, NH, SEQ], F16).ap()
    table = [nc.dram_tensor(f"table{i}", [CHUNK, 2 * D], F16).ap() for i in range(2)]
    ytab = [nc.dram_tensor(f"ytab{i}", [SLOT_TILES * P, D], F32).ap() for i in range(2)]

    with ExitStack() as ctx:
        def sb(n, s, d=F32):
            return ctx.enter_context(nc.sbuf_tensor(n, s, d))

        def ps(n, s, d=F32):
            return ctx.enter_context(nc.psum_tensor(n, s, d))

        def sem(n):
            return ctx.enter_context(nc.semaphore(n))

        def wait(eng, s, v):
            if v > 0:
                eng.wait_ge(s, v)

        xs = sb("xs", [P, NT, D])
        wa_s = sb("wa_s", [P, D]); wc = sb("wc", [P, D]); cb = sb("cb", [1, D]); ba_s = sb("ba_s", [P, 1])
        wq_s = sb("wq_s", [P, D]); wk_s = sb("wk_s", [P, D]); wv_s = sb("wv_s", [P, D]); wo_s = sb("wo_s", [P, D])
        bq_s = sb("bq_s", [P, 1]); bk_s = sb("bk_s", [P, 1]); bv_s = sb("bv_s", [1, D]); bo_s = sb("bo_s", [1, D])
        ga_s = sb("ga_s", [P, 1]); be_s = sb("be_s", [P, 1]); rw_s = sb("rw_s", [P, E])
        ga_row = sb("ga_row", [P, D]); be_row = sb("be_row", [P, D])
        wff = sb("wff", [P, E, 4, H], F16)
        ident = sb("ident", [P, P]); ident16 = sb("ident16", [P, P], F16)
        tri = sb("tri", [P, P]); ones_row = sb("ones_row", [1, P]); ones_col = sb("ones_col", [P, 1])
        before16 = sb("before16", [P, P], F16); ones16 = sb("ones16", [P, P], F16)
        lane16 = sb("lane16", [P, P], F16); tile16 = sb("tile16", [P, SLOT_TILES], F16); token_id = sb("token_id", [P, CT])
        steps = sb("steps", [P, E, CT]); upto = sb("upto", [P, E, E]); tiles3 = sb("tiles3", [1, SLOT_TILES, E])
        prefer = sb("prefer", [P, CT, E])
        mband = sb("mband", [P, 256], F16); mlower = sb("mlower", [P, P], F16)
        mhalf = sb("mhalf", [P, 2, CT])
        st = sb("st", [P, CT, 6]); lsum = sb("lsum", [P, CT]); ldif = sb("ldif", [P, CT]); lm2 = sb("lm2", [P, CT])
        lvar = sb("lvar", [P, CT]); mean = sb("mean", [P, CT]); ve = sb("ve", [P, 2, CT]); r0 = sb("r0", [P, 2, CT])
        newt = sb("newt", [P, 2, CT]); rr = sb("rr", [P, 2, CT]); r1p = sb("r1p", [P, CT]); nmr = sb("nmr", [P, CT])
        zr = sb("zr", [P, 2, TPB, D]); zT = sb("zT", [P, 2, SEQ])
        lg = sb("lg", [P, CT, E]); pr = sb("pr", [P, CT, E]); key = sb("key", [P, CT, E]); oh = sb("oh", [P, 2, CT, E])
        lg2 = sb("lg2", [P, CT, E]); rm = sb("rm", [P, 4, CT]); c16 = sb("c16", [P, CT, E], F16)
        wk2 = sb("wk2", [P, 2, 2, CT]); pwork = sb("pwork", [P, 2, CT, E])
        cnt = sb("cnt", [P, E]); ge3 = sb("ge3", [P, E, CT]); te = sb("te", [P, E]); en = sb("en", [P, E]); off = sb("off", [P, E])
        posb = sb("posb", [P, CT, E]); pos = sb("pos", [P, 2, CT])
        posi = sb("posi", [P, 2, 2, CT], U32); lani = sb("lani", [P, 2, CT], I32); tili = sb("tili", [P, 2, CT], I32)
        lanf = sb("lanf", [P, 2, CT]); tilf = sb("tilf", [P, 2, CT])
        ohl = sb("ohl", [P, 2, CT, P], F16); oht = sb("oht", [P, 2, CT, SLOT_TILES], F16)
        idx = sb("idx", [P, 2, SLOT_TILES], U32)
        eg3 = sb("eg3", [1, SLOT_TILES, E]); egf = sb("egf", [1, SLOT_TILES]); eid = sb("eid", [1, 2, SLOT_TILES], I32)
        xnb = sb("xnb", [P, 2, TPB, D]); tb = sb("tb", [P, 2, TPB, 2, D], F16)
        xg = sb("xg", [P, G, 2, D], F16); xT = sb("xT", [P, 3, 2 * P], F16)
        g32 = sb("g32", [P, 3, H]); gh = sb("gh", [P, 3, H], F16); gl = sb("gl", [P, 3, H], F16)
        ysb = sb("ysb", [P, G, D]); cg = sb("cg", [P, 2, TPB, 2, D])
        hi = sb("hi", [P, 2, SEQ], F16); lo = sb("lo", [P, 2, SEQ], F16)
        qz = sb("qz", [P, 3, NH, SEQ], F16); kst = sb("kst", [P, 3, SETS, SEQ], F16)
        vp = sb("vp", [P, 3, TPB, VROW]); vsum = sb("vsum", [P, 3, 1]); vrow = sb("vrow", [1, D])
        mx = sb("mx", [P, TPB, NH]); mT = sb("mT", [NH, SEQ], F16)
        pT = sb("pT", [P, 3, 4 * 256])
        uT = ohl[:].rearrange("p k t n -> p (k t n)").bitcast(F32).rearrange("p (s n) -> p s n", s=SETS)
        cx = g32[:, 0, :].rearrange("p (t d) -> p t d", t=TPB)
        cT = g32[:, 1, :]
        rden = lg[:, 0:TPB * NH // E, :].rearrange("p (t a) e -> p t (a e)", t=TPB)
        stage = qz[:].rearrange("p u h n -> p (u h n)")[:, 0:4 * E * H].bitcast(F32).rearrange("p (w n) -> p w n", w=2)

        bank = [ps(f"bank{i}", [P, 512]) for i in range(2)]
        sbank = ps("sbank", [P, 2, 512])
        stbank = ps("stbank", [P, 4, 512])
        LG = bank[1][:, 0:CT * E].rearrange("p (t e) -> p t e", e=E)
        RK = bank[1][:, CT * E:2 * CT * E].rearrange("p (t e) -> p t e", e=E)
        CN = bank[1][:, 2 * CT * E:2 * CT * E + E]
        IX = bank[1][:, 2 * CT * E + E:2 * CT * E + E + SLOT_TILES]
        xbank = [sbank[:, i, 0:P].bitcast(F16) for i in range(2)]
        hbank = [stbank[:, i, :] for i in range(2)]
        ybank = [stbank[:, 2 + i, 0:2 * D] for i in range(2)]

        s_x = [sem(f"x{b}_loaded") for b in range(B)]; s_w = sem("weights_loaded")
        s_wff = [sem(f"w{i}_staged") for i in range(2)]; s_wh = sem("weights_high"); s_wl = sem("weights_low")
        s_const = sem("constants_made"); s_chain = sem("pool_chain"); s_wcp = sem("wc_psum"); s_wcs = sem("wc_ready")
        s_ve = sem("variance_ready"); s_r0 = sem("rsqrt_guess")
        s_z = sem("z_ready"); s_zp = sem("z_transposed"); s_zt = sem("zt_ready"); s_ztf = sem("zt_used")
        s_am = sem("linear_psum"); s_aa = sem("linear_added")
        s_xn = sem("xn_ready"); s_xh = sem("xn_high"); s_tb = sem("table_rows_ready")
        s_tbd = [sem(f"table_rows_stored{i}") for i in range(2)]
        s_lg = sem("logits_psum"); s_lc = sem("logits_centred"); s_pe = sem("probs_exp")
        s_c16 = sem("choices_ready"); s_cn = sem("counts_psum"); s_oh = sem("slot_onehots"); s_ixp = sem("slots_psum")
        s_idx = sem("slot_indices_ready")
        s_g = [sem(f"gathered{i}") for i in range(G)]; s_xp = sem("x_transposed"); s_xt = sem("xt_ready")
        s_h = sem("h_psum"); s_gh = sem("g_ready"); s_gl = sem("g_low_ready"); s_y = sem("y_psum"); s_yc = sem("y_copied")
        s_ys = [sem(f"y_stored{i}") for i in range(G)]; s_cg = [sem(f"y_gathered{i}") for i in range(2)]; s_cd = sem("combined")
        s_qk = sem("qk_psum"); s_hi = sem("hi_ready"); s_lo = sem("lo_ready"); s_vm = sem("v_psum"); s_v = sem("v_ready")
        s_vs = sem("vsum_psum"); s_vsr = sem("vsum_ready")
        s_dump = sem("qk_dumped"); s_stk = [sem(f"stacks_loaded{i}") for i in range(2)]; s_zero = sem("stacks_zeroed")
        s_s = sem("s_psum"); s_red = sem("s_reduced"); s_mtp = sem("max_transposed"); s_mt = sem("max_ready")
        s_md = sem("max_dumped"); s_mr = sem("max_row_loaded")
        s_st = sem("st_psum"); s_e = sem("exp_ready"); s_pm = sem("p_masked"); s_pmc = sem("p_mask_half")
        s_pv = sem("pv_done"); s_u = sem("u_copied")
        s_ut = sem("u_transposed"); s_cx = sem("ctx_ready"); s_cxp = sem("ctx_transposed"); s_ct = sem("ct_ready")
        s_o = sem("o_psum"); s_oa = sem("o_added"); s_out = sem("stored")

        block = ctx.enter_context(nc.Block())
        N_W = 15
        N_CONST = 1

        def z_linear(b):
            return b if b < BPC else 2 * BPC + (b - BPC)

        def z_router(cc, i):
            return (BPC, 3 * BPC, 6 * BPC, 7 * BPC)[cc] + i

        def z_attn(b):
            return 4 * BPC + b

        XSTEPS = SLOT_TILES + 4

        def tile_of(cc, t):
            return SLOT_TILES * cc + t

        def combine_at(s):
            return (s - 4) // 9 if s >= 4 and (s - 4) % 9 == 0 and (s - 4) // 9 < BPC else None

        def layer_pass(a_piece, r_piece, x_step, combine, layer):
            c0 = CHUNKS * layer
            for k in range(PIECES_R):
                r_piece(c0, k)
            for s in range(XSTEPS):
                x_step(c0, s)
                if layer == 0:
                    if s < PIECES_A:
                        a_piece(1, s)
                    elif s < PIECES_A + PIECES_R:
                        r_piece(c0 + 1, s - PIECES_A)
                elif s < PIECES_R:
                    r_piece(c0 + 1, s)
            for s in range(XSTEPS):
                x_step(c0 + 1, s)
                if combine_at(s) is not None:
                    combine(layer, combine_at(s))

        @block.sync
        def _(sp):
            def load_x(b):
                sp.dma_start(xs[:, TPB * b:TPB * b + TPB, :], x_t[:, TPB * b:TPB * b + TPB, :]).then_inc(s_x[b], 16)
            for b in range(BPC):
                load_x(b)
            for d, s in ((wa_s, wa), (ba_s, ba), (ga_s, gamma), (be_s, beta), (rw_s, rw), (wq_s, wq), (wk_s, wk), (wv_s, wv),
                         (wo_s, wo), (bq_s, bq), (bk_s, bk), (bv_s, bv), (bo_s, bo)):
                sp.dma_start(d[:], s).then_inc(s_w, 16)
            for d, s in ((ga_row, gamma), (be_row, beta)):
                sp.dma_start(d[:], s.rearrange("d a -> a d").to_broadcast([P, D])).then_inc(s_w, 16)
            for w, src in ((0, w1.rearrange("e d f -> d e f")), (1, w2.rearrange("e (c p) d -> p (e c) d", p=P))):
                sp.dma_start(stage[:, w, :].rearrange("p (a n) -> p a n", n=src.shape[2]), src).then_inc(s_wff[w], 16)
            for b in range(BPC, B):
                load_x(b)

            def nothing(*_):
                pass

            def r_piece(cc, k):
                if 7 <= k <= 10:
                    i = k - 7
                    if i == 0:
                        wait(sp, s_xp, SLOT_TILES * (cc - 1))
                    sp.wait_ge(s_tb, BPC * cc + i + 1)
                    sp.dma_start(table[cc % 2][SEQ * i:SEQ * (i + 1), :].rearrange("(t p) n -> p t n", p=P),
                                 tb[:, i % 2].rearrange("p t a d -> p t (a d)")).then_inc(s_tbd[i % 2], 16)

            def x_step(cc, s):
                t = s - 4
                if t >= 0:
                    i = tile_of(cc, t)
                    if t == 0:
                        wait(sp, s_cd, BPC * (cc - 1))
                    sp.wait_ge(s_yc, i + 1)
                    sp.dma_start(ytab[cc % 2][P * t:P * t + P, :], ysb[:, i % G, :]).then_inc(s_ys[i % G], 16)

            def store_out(layer, b):
                if layer == 1:
                    sp.wait_ge(s_cd, B + b + 1)
                    sp.dma_start(out_t[:, TPB * b:TPB * b + TPB, :], xs[:, TPB * b:TPB * b + TPB, :]).then_inc(s_out, 16)

            layer_pass(nothing, r_piece, x_step, store_out, 0)

            def load_stacks(b):
                par, slot = b % 2, b % 3
                wait(sp, s_s, UNITS * (b - 1))
                for i in range(2):
                    sp.wait_ge(s_hi, 2 * b + i + 1)
                    sp.dma_start(dumps[par, 2 * i], hi[:, i, :]).then_inc(s_dump, 16)
                    sp.wait_ge(s_lo, 2 * b + i + 1)
                    sp.dma_start(dumps[par, 2 * i + 1], lo[:, i, :]).then_inc(s_dump, 16)
                sp.wait_ge(s_dump, 64 * (b + 1))
                sp.wait_ge(s_zero, 1)
                wait(sp, s_st, UNITS * (b - 2))
                for i, parts in ((0, (0, 0, 1)), (1, (0, 1, 0))):
                    for g in range(4):
                        for c in range(3):
                            src = dumps[par, 2 * i + parts[c]].rearrange("(g s j) n -> g j s n", g=4, s=SETS)[g]
                            r = 32 * g + DK * c
                            dst = (qz[r:r + DK, slot, g * SETS:(g + 1) * SETS, :] if i == 0 else kst[r:r + DK, slot, :, :])
                            sp.dma_start(dst, src).then_inc(s_stk[par], 16)

            load_stacks(0)
            load_stacks(1)
            for b in range(B):
                sp.wait_ge(s_mt, b + 1)
                sp.dma_start(mdump[b % 2], mT[:]).then_inc(s_md, 16)
                sp.wait_ge(s_md, 16 * (b + 1))
                sp.dma_start(qz[P - 1:P, b % 3, :, :], mdump[b % 2].rearrange("(a h) n -> a h n", a=1)).then_inc(s_mr, 16)
                if b + 2 < B:
                    load_stacks(b + 2)
            layer_pass(nothing, r_piece, x_step, store_out, 1)
            for b in range(BPC, B):
                store_out(1, b)
            sp.wait_ge(s_out, 16 * B)

        @block.gpsimd
        def _(pool):
            g = nc.gpsimd
            n = [0]

            def made(ins):
                n[0] += 1
                ins.then_inc(s_chain, 1)

            for t, v in ((ident, 0.0), (tri, 1.0), (ones_row, 1.0), (ones_col, 1.0), (before16, 1.0), (ones16, 1.0),
                         (upto, 1.0), (mhalf, -0.5)):
                made(g.memset(t[:], v))
            any_ = dict(allow_small_or_imprecise_dtypes=True)
            made(g.iota(lane16[:], pattern=[[1, P]], base=0, channel_multiplier=0, **any_))
            made(g.iota(tile16[:], pattern=[[1, SLOT_TILES]], base=0, channel_multiplier=0, **any_))
            made(g.iota(token_id[:], pattern=[[P, CT]], base=0, channel_multiplier=1, **any_))
            made(g.iota(steps[:], pattern=[[0, E], [P, CT]], base=0, channel_multiplier=0, **any_))
            made(g.iota(tiles3[:], pattern=[[1, SLOT_TILES], [0, E]], base=0, channel_multiplier=0, **any_))
            made(g.iota(prefer[:], pattern=[[0, CT], [-1, E]], base=E, channel_multiplier=0, **any_))
            pool.wait_ge(s_chain, n[0])
            made(g.affine_select(out=ident[:], in_=ident[:], compare_op=ALU.not_equal, fill=1.0, base=0,
                                 pattern=[[1, P]], channel_multiplier=-1))
            made(g.affine_select(out=tri[:], in_=tri[:], compare_op=ALU.is_ge, fill=0.0, base=0,
                                 pattern=[[1, P]], channel_multiplier=-1))
            made(g.affine_select(out=before16[:], in_=before16[:], compare_op=ALU.is_ge, fill=0.0, base=-1,
                                 pattern=[[1, P]], channel_multiplier=-1))
            made(g.affine_select(out=upto[:], in_=upto[:], compare_op=ALU.is_ge, fill=0.0, base=0,
                                 pattern=[[1, E], [-1, E]], channel_multiplier=0))
            pool.wait_ge(s_chain, n[0])
            g.tensor_copy(ident16[:], ident[:]).then_inc(s_const, 1)

            def pow_(i):
                pool.wait_ge(s_ve, i + 1)
                g.tensor_tensor(r0[:], ve[:], mhalf[:], ALU.pow).then_inc(s_r0, 1)

            def a_piece(c, k):
                if k == 4:
                    pow_(2 * c)

            def r_piece(cc, k):
                if k == 4:
                    pow_((1, 3, 4 + B, 5 + B)[cc])

            def x_step(cc, s):
                if s == 0:
                    pool.wait_ge(s_idx, cc + 1)
                    for i in range(2):
                        pool.wait_ge(s_tbd[i], 16 * 2 * (cc + 1))
                if s < SLOT_TILES:
                    i = tile_of(cc, s)
                    wait(pool, s_xp, i - G + 1)
                    g.indirect_dma_start(xg[:, i % G].rearrange("p a d -> p (a d)"), None, table[cc % 2],
                                         bass.IndirectOffsetOnAxis(ap=idx[:, cc % 2, s:s + 1], axis=0)).then_inc(s_g[i % G], 16)

            def gather_back(layer, b):
                cc = CHUNKS * layer + b // BPC
                if b % BPC == 0:
                    last = tile_of(cc + 1, 0)
                    for i in range(G):
                        pool.wait_ge(s_ys[i], 16 * ((last - 1 - i) // G + 1))
                wait(pool, s_cd, B * layer + b - 1)
                for t in range(TPB):
                    for k in range(2):
                        at = (b % BPC) * TPB + t
                        g.indirect_dma_start(cg[:, b % 2, t, k, :], None, ytab[cc % 2],
                                             bass.IndirectOffsetOnAxis(ap=posi[:, cc % 2, k, at:at + 1], axis=0)
                                             ).then_inc(s_cg[b % 2], 16)

            a_piece(0, 4)
            made(g.memset(kst[:], 0.0))
            made(g.memset(vp[:], 1.0))
            made(g.memset(mband[:], 0.0))
            made(g.memset(mlower[:], 0.0))
            pool.wait_ge(s_chain, n[0])
            made(g.affine_select(out=mband[:], in_=mband[:], compare_op=ALU.is_ge, fill=MASKED, base=0,
                                 pattern=[[1, 256]], channel_multiplier=-1))
            made(g.affine_select(out=mlower[:], in_=mlower[:], compare_op=ALU.is_ge, fill=MASKED, base=0,
                                 pattern=[[-1, P]], channel_multiplier=1))
            made(g.affine_select(out=kst[:], in_=kst[:], compare_op=ALU.not_equal, fill=1.0, base=-(P - 1),
                                 pattern=[[0, 3], [0, SETS], [0, SEQ]], channel_multiplier=1))
            pool.wait_ge(s_chain, n[0])
            made(g.affine_select(out=mband[:], in_=mband[:], compare_op=ALU.is_ge, fill=MASKED, base=P,
                                 pattern=[[-1, 256]], channel_multiplier=1))
            pool.wait_ge(s_chain, n[0])
            layer_pass(a_piece, r_piece, x_step, gather_back, 0)
            pool.wait_ge(s_wl, 2)
            pool.wait_ge(s_wh, 2)
            g.memset(qz[:].bitcast(F32), 0.0).then_inc(s_zero, 1)

            def mask(b, j):
                kt = j % TPB
                w = 256 if kt < TPB - 1 else 128
                i = UNITS * b + j
                pool.wait_ge(s_e, i + 1)
                p = pT[:, i % 3, 0:4 * w].rearrange("p (h q) -> p h q", q=w)
                ins = g.affine_select(out=p[:, :, 0:P], in_=p[:, :, 0:P], compare_op=ALU.is_ge, fill=0.0, base=0,
                                      pattern=[[0, 4], [1, P]], channel_multiplier=-1)
                if w == 256:
                    ins = g.affine_select(out=p[:, :, P:256], in_=p[:, :, P:256], compare_op=ALU.is_ge, fill=0.0, base=0,
                                          pattern=[[0, 4], [-1, P]], channel_multiplier=1)
                ins.then_inc(s_pm, 1)

            pow_(4)
            pow_(5)
            for b in range(B):
                for j in range(UNITS):
                    mask(b, j)
                    if j == 0 and b + 2 < B:
                        pow_(4 + b + 2)
                    if j == 6 and BPC <= b + 3 < B:
                        gather_back(0, b + 3)
            layer_pass(a_piece, r_piece, x_step, gather_back, 1)
            for b in range(BPC, B):
                gather_back(1, b)

        @block.vector
        def _(dve):
            v = nc.vector

            def stats(tile, slot):
                v.bn_stats(st[:, slot, :], xs[:, tile, :])

            def norm_begin(nt):
                dve.drain()
                v.tensor_tensor(lsum[:, 0:nt], st[:, 0:nt, 1], st[:, 0:nt, 4], ALU.add)
                v.tensor_tensor(ldif[:, 0:nt], st[:, 0:nt, 1], st[:, 0:nt, 4], ALU.subtract)
                v.tensor_tensor(lm2[:, 0:nt], st[:, 0:nt, 2], st[:, 0:nt, 5], ALU.add)
                dve.drain()
                v.tensor_scalar(mean[:, 0:nt], lsum[:, 0:nt], 0.5, None, ALU.mult)
                v.tensor_tensor(ldif[:, 0:nt], ldif[:, 0:nt], ldif[:, 0:nt], ALU.mult)
                v.tensor_scalar(lm2[:, 0:nt], lm2[:, 0:nt], 1.0 / D, None, ALU.mult)
                dve.drain()
                v.scalar_tensor_tensor(out=lvar[:, 0:nt], in0=ldif[:, 0:nt], scalar=0.25, in1=lm2[:, 0:nt],
                                       op0=ALU.mult, op1=ALU.add)
                dve.drain()
                v.tensor_scalar(ve[:, 0, 0:nt], lvar[:, 0:nt], EPS, None, ALU.add)
                v.tensor_scalar(ve[:, 1, 0:nt], lvar[:, 0:nt], 1.0 + EPS, EPS * EPS, ALU.mult, ALU.add).then_inc(s_ve, 1)

            def norm_end(i):
                dve.wait_ge(s_r0, i + 1)
                v.tensor_tensor(newt[:], r0[:], r0[:], ALU.mult)
                dve.drain()
                v.tensor_tensor(newt[:], newt[:], ve[:], ALU.mult)
                dve.drain()
                v.tensor_scalar(newt[:], newt[:], -0.5, 1.5, ALU.mult, ALU.add)
                dve.drain()
                v.tensor_tensor(rr[:], r0[:], newt[:], ALU.mult)
                dve.drain()

            def normalise(n, tile, slot, which):
                wait(dve, s_zp, n - 1)
                for t in range(TPB):
                    ins = v.tensor_scalar(zr[:, n % 2, t, :], xs[:, tile + t, :], mean[:, slot + t:slot + t + 1],
                                          rr[:, which, slot + t:slot + t + 1], ALU.subtract, ALU.mult)
                ins.then_inc(s_z, 1)

            def flat(b):
                return xs[:, TPB * b:TPB * b + TPB, :].rearrange("p t d -> p (t d)")

            def a_piece(c, k):
                if k < BPC:
                    b = BPC * c + k
                    dve.wait_ge(s_x[b], 16)
                    for t in range(TPB):
                        stats(TPB * b + t, TPB * k + t)
                elif k == 4:
                    norm_begin(CT)
                elif k == 5:
                    norm_end(2 * c)
                elif k < 6 + BPC:
                    normalise(z_linear(BPC * c + k - 6), CT * c + TPB * (k - 6), TPB * (k - 6), 0)
                if k > 6:
                    b = BPC * c + k - 7
                    dve.wait_ge(s_am, b + 1)
                    v.tensor_tensor(flat(b), flat(b), bank[1][:, :], ALU.add).then_inc(s_aa, 1)

            def r_piece(cc, k):
                c, cp = cc % CHUNKS, cc % 2

                def over_e(a):
                    return a.unsqueeze(2).to_broadcast([P, CT, E])

                if k < BPC:
                    if k == 0:
                        dve.drain()
                    for t in range(TPB):
                        stats(CT * c + TPB * k + t, TPB * k + t)
                elif k == 4:
                    norm_begin(CT)
                elif k == 5:
                    norm_end((1, 3, 4 + B, 5 + B)[cc])
                    v.tensor_scalar(r1p[:], rr[:, 0, :], 1.0, None, ALU.add)
                    v.scalar_tensor_tensor(out=nmr[:], in0=mean[:], scalar=-1.0, in1=rr[:, 0, :], op0=ALU.mult, op1=ALU.mult)
                elif k <= 10:
                    i = k - 6
                    if i < BPC:
                        n = z_router(cc, i)
                        normalise(n, CT * c + TPB * i, TPB * i, 1)
                        dve.drain()
                        xn = xnb[:, i % 2]
                        v.tensor_tensor(xn, zr[:, n % 2], ga_row[:].unsqueeze(1).to_broadcast([P, TPB, D]), ALU.mult)
                        dve.drain()
                        v.tensor_tensor(xn, xn, be_row[:].unsqueeze(1).to_broadcast([P, TPB, D]), ALU.add).then_inc(s_xn, 1)
                    if i:
                        j = i - 1
                        dve.wait_ge(s_xh, BPC * cc + j + 1)
                        v.tensor_tensor(tb[:, j % 2, :, 1, :], xnb[:, j % 2], tb[:, j % 2, :, 0, :],
                                        ALU.subtract).then_inc(s_tb, 1)
                elif k == 11:
                    for t in range(CT):
                        tile = xs[:, CT * c + t, :]
                        v.tensor_scalar(tile, tile, r1p[:, t:t + 1], nmr[:, t:t + 1], ALU.mult, ALU.add)
                elif k == 12:
                    dve.wait_ge(s_lg, cc + 1)
                    v.tensor_copy(lg[:], LG)
                    dve.drain()
                    v.tensor_reduce(rm[:, 0, :], lg[:], AX.X, ALU.max)
                    dve.drain()
                    v.tensor_tensor(lg[:], lg[:], over_e(rm[:, 0, :]), ALU.subtract).then_inc(s_lc, 1)
                    dve.drain()
                    v.scalar_tensor_tensor(out=key[:], in0=lg[:], scalar=0.0, in1=prefer[:], op0=ALU.is_equal, op1=ALU.mult)
                    dve.drain()
                    v.tensor_reduce(rm[:, 1, :], key[:], AX.X, ALU.max)
                    dve.drain()
                    v.tensor_tensor(oh[:, 0], key[:], over_e(rm[:, 1, :]), ALU.is_equal)
                    dve.drain()
                elif k == 13:
                    v.scalar_tensor_tensor(out=lg2[:], in0=oh[:, 0], scalar=-1e30, in1=lg[:], op0=ALU.mult, op1=ALU.add)
                    dve.drain()
                    v.tensor_reduce(rm[:, 2, :], lg2[:], AX.X, ALU.max)
                    dve.drain()
                    v.tensor_tensor(key[:], lg2[:], over_e(rm[:, 2, :]), ALU.is_equal)
                    dve.drain()
                    v.tensor_tensor(key[:], key[:], prefer[:], ALU.mult)
                    dve.drain()
                    v.tensor_reduce(rm[:, 1, :], key[:], AX.X, ALU.max)
                    dve.drain()
                    v.tensor_tensor(oh[:, 1], key[:], over_e(rm[:, 1, :]), ALU.is_equal)
                    dve.drain()
                    v.tensor_tensor(c16[:], oh[:, 0], oh[:, 1], ALU.add).then_inc(s_c16, 1)
                elif k == 14:
                    dve.wait_ge(s_pe, cc + 1)
                    v.tensor_reduce(rm[:, 3, :], pr[:], AX.X, ALU.add)
                    for i in range(2):
                        v.tensor_tensor(pwork[:, i], oh[:, i], pr[:], ALU.mult)
                    dve.drain()
                    v.reciprocal(rm[:, 3, :], rm[:, 3, :])
                    v.tensor_reduce(wk2[:, cp], pwork[:], AX.X, ALU.add)
                    dve.drain()
                    v.scalar_tensor_tensor(out=wk2[:, cp], in0=wk2[:, cp], scalar=1.0 / WSCALE,
                                           in1=rm[:, 3, :].unsqueeze(1).to_broadcast([P, 2, CT]), op0=ALU.mult, op1=ALU.mult)
                elif k == 15:
                    dve.wait_ge(s_cn, cc + 1)
                    v.tensor_copy(cnt[:], CN)
                    dve.drain()
                    v.tensor_tensor(ge3[:], cnt[:].unsqueeze(2).to_broadcast([P, E, CT]), steps[:], ALU.is_gt)
                    dve.drain()
                    v.tensor_reduce(te[:], ge3[:], AX.X, ALU.add)
                    dve.drain()
                    v.tensor_tensor(ge3[:, :, 0:E], te[:].unsqueeze(1).to_broadcast([P, E, E]), upto[:], ALU.mult)
                    dve.drain()
                    v.tensor_reduce(en[:], ge3[:, :, 0:E], AX.X, ALU.add)
                    dve.drain()
                    v.tensor_tensor(off[:], en[:], te[:], ALU.subtract)
                    dve.drain()
                    v.tensor_scalar(off[:], off[:], float(P), None, ALU.mult)
                    dve.drain()
                    v.tensor_tensor(posb[:], RK, off[:].unsqueeze(1).to_broadcast([P, CT, E]), ALU.add)
                    dve.drain()
                    for i in range(2):
                        v.tensor_tensor(pwork[:, i], oh[:, i], posb[:], ALU.mult)
                    dve.drain()
                    v.tensor_reduce(pos[:], pwork[:], AX.X, ALU.add)
                    dve.drain()
                elif k == 16:
                    pi = posi[:, cp]
                    v.tensor_copy(pi, pos[:])
                    dve.drain()
                    v.tensor_scalar(lani[:], pi.bitcast(I32), P - 1, None, ALU.bitwise_and)
                    v.tensor_scalar(tili[:], pi.bitcast(I32), P.bit_length() - 1, None, ALU.arith_shift_right)
                    v.tensor_tensor(eg3[:], tiles3[:], en[0:1, :].unsqueeze(1).to_broadcast([1, SLOT_TILES, E]), ALU.is_ge)
                    dve.drain()
                    v.tensor_copy(lanf[:], lani[:])
                    v.tensor_copy(tilf[:], tili[:])
                    v.tensor_reduce(egf[:], eg3[:], AX.X, ALU.add)
                    dve.drain()
                    v.tensor_scalar(eid[:, cp, :], egf[:], float(E - 1), None, ALU.min)
                elif k <= 20:
                    for t in range(TPB * (k - 17), TPB * (k - 17) + TPB):
                        for i in range(2):
                            v.tensor_scalar(ohl[:, i, t, :], lane16[:], lanf[:, i, t:t + 1], None, ALU.is_equal)
                            ins = v.tensor_scalar(oht[:, i, t, :], tile16[:], tilf[:, i, t:t + 1], token_id[:, t:t + 1],
                                                  ALU.is_equal, ALU.mult)
                    ins.then_inc(s_oh, 1)
                else:
                    dve.wait_ge(s_ixp, cc + 1)
                    v.tensor_copy(idx[:, cp, :], IX).then_inc(s_idx, 1)

            def x_step(cc, s):
                if s < SLOT_TILES:
                    i = tile_of(cc, s)
                    dve.wait_ge(s_xp, i + 1)
                    wait(dve, s_h, i - 2)
                    v.tensor_copy(xT[:, i % 3, :], xbank[i % 2]).then_inc(s_xt, 1)
                if 0 <= s - 4 < SLOT_TILES:
                    i = tile_of(cc, s - 4)
                    dve.wait_ge(s_y, i + 1)
                    wait(dve, s_ys[i % G], 16 * (i // G))
                    v.tensor_reduce(ysb[:, i % G, :], ybank[i % 2].rearrange("p (a d) -> p d a", a=2), AX.X, ALU.add).then_inc(s_yc, 1)
                if 0 <= s - 2 < SLOT_TILES:
                    i = tile_of(cc, s - 2)
                    dve.wait_ge(s_gh, i + 1)
                    wait(dve, s_y, i - 2)
                    v.tensor_tensor(gl[:, i % 3, :], g32[:, i % 3, :], gh[:, i % 3, :], ALU.subtract).then_inc(s_gl, 1)

            def combine(layer, b):
                cp = (CHUNKS * layer + b // BPC) % 2
                dve.wait_ge(s_cg[b % 2], 16 * 2 * TPB * (B // 2 * layer + b // 2 + 1))
                for k in range(2):
                    for t in range(TPB):
                        tile = xs[:, TPB * b + t, :]
                        at = (b % BPC) * TPB + t
                        ins = v.scalar_tensor_tensor(out=tile, in0=cg[:, b % 2, t, k, :], scalar=wk2[:, cp, k, at:at + 1],
                                                     in1=tile, op0=ALU.mult, op1=ALU.add)
                    if k == 0:
                        dve.drain()
                ins.then_inc(s_cd, 1)

            def split_low(w):
                dve.wait_ge(s_wh, w + 1)
                v.scalar_tensor_tensor(out=wff[:, :, 2 * w + 1, :], in0=stage[:, w, :].rearrange("p (e n) -> p e n", e=E),
                                       scalar=WSCALE, in1=wff[:, :, 2 * w, :], op0=ALU.mult, op1=ALU.subtract).then_inc(s_wl, 1)

            dve.wait_ge(s_w, 16 * N_W)
            for k in range(PIECES_A):
                a_piece(0, k)
            split_low(0)
            split_low(1)
            layer_pass(a_piece, r_piece, x_step, combine, 0)

            def front(b, j):
                if j == 0:
                    if b >= BPC:
                        combine(0, b)
                    dve.drain()
                    for t in range(TPB):
                        stats(TPB * b + t, t)
                    norm_begin(TPB)
                elif j == 2:
                    norm_end(4 + b)
                    normalise(z_attn(b), TPB * b, 0, 0)
                elif j in (5, 8):
                    i, bias = (0, bq_s) if j == 5 else (1, bk_s)
                    dve.wait_ge(s_hi, 2 * b + i + 1)
                    wait(dve, s_dump, 64 * b)
                    v.scalar_tensor_tensor(out=lo[:, i, :], in0=bank[1][:, :], scalar=bias[:, 0:1], in1=hi[:, i, :],
                                           op0=ALU.add, op1=ALU.subtract).then_inc(s_lo, 1)

            def reduce(b, j):
                s, qt = j // TPB, j % TPB
                dve.wait_ge(s_s, UNITS * b + j + 1)
                w = 256 if qt else 128
                m = mband if qt else mlower
                if j == 0:
                    wait(dve, s_mtp, b)
                for g in range(4):
                    src = sbank[:].rearrange("p a n -> p (a n)")[:, w * g:w * g + w]
                    ins = v.tensor_tensor_reduce(out=src, in0=src, in1=m[:], scale=1.0, scalar=-3e38, op0=ALU.add,
                                                 op1=ALU.max, accum_out=mx[:, qt, 4 * s + g:4 * s + g + 1])
                ins.then_inc(s_red, 1)

            def back(b):
                for qt in range(TPB):
                    dve.wait_ge(s_ut, TPB * b + qt + 1)
                    u = sbank[:, qt % 2, :].rearrange("p (h r) -> p h r", r=32)
                    v.reciprocal(rden[:, qt, :], u[:, :, DK])
                    dve.drain()
                    v.tensor_tensor(cx[:, qt, :].rearrange("p (h j) -> p h j", j=DK), u[:, :, 0:DK],
                                    rden[:, qt, :].unsqueeze(2).to_broadcast([P, NH, DK]), ALU.mult).then_inc(s_cx, 1)
                dve.wait_ge(s_o, b + 1)
                v.tensor_tensor(flat(b), flat(b), bank[1][:, :], ALU.add).then_inc(s_oa, 1)

            for b in range(2):
                for j in range(UNITS):
                    front(b, j)
            for j in range(UNITS):
                reduce(0, j)
            for b in range(B):
                if b:
                    back(b - 1)
                for j in range(UNITS):
                    if b + 1 < B:
                        reduce(b + 1, j)
                    if b + 2 < B:
                        front(b + 2, j)
            back(B - 1)
            dve.drain()
            layer_pass(a_piece, r_piece, x_step, combine, 1)
            for b in range(BPC, B):
                combine(1, b)

        @block.scalar
        def _(act):
            a = nc.scalar

            def evac_z(n, affine=False):
                act.wait_ge(s_zp, n + 1)
                wait(act, s_ztf, n - 1)
                src = bank[1] if z_attn(0) <= n < z_attn(B) else bank[0]
                if affine:
                    a.activation(zT[:, n % 2, :], src[:, :], ACT.Identity, scale=ga_s[:, 0:1],
                                 bias=be_s[:, 0:1]).then_inc(s_zt, 1)
                else:
                    a.activation(zT[:, n % 2, :], src[:, :], ACT.Copy).then_inc(s_zt, 1)

            def a_piece(c, k):
                if 6 <= k < 6 + BPC:
                    evac_z(z_linear(BPC * c + k - 6))

            def r_piece(cc, k):
                if 6 <= k < 6 + BPC:
                    i = k - 6
                    act.wait_ge(s_xn, BPC * cc + i + 1)
                    if i >= 2:
                        act.wait_ge(s_tbd[i % 2], 16 * (2 * cc + 1))
                    elif cc:
                        act.wait_ge(s_tbd[i % 2], 16 * 2 * cc)
                    a.activation(tb[:, i % 2, :, 0, :], xnb[:, i % 2], ACT.Copy).then_inc(s_xh, 1)
                    evac_z(z_router(cc, i), True)
                elif k == 12:
                    act.wait_ge(s_lc, cc + 1)
                    a.activation(pr[:], lg[:], ACT.Exp, scale=1.0 / TEMP).then_inc(s_pe, 1)

            def x_step(cc, s):
                if 0 <= s - 2 < SLOT_TILES:
                    i = tile_of(cc, s - 2)
                    act.wait_ge(s_h, i + 1)
                    wait(act, s_gl, i - 2)
                    wait(act, s_y, i - 2)
                    a.activation(g32[:, i % 3, :], hbank[i % 2], ACT.Silu, scale=1.0 / WSCALE)
                    a.activation(gh[:, i % 3, :], hbank[i % 2], ACT.Silu, scale=1.0 / WSCALE).then_inc(s_gh, 1)

            def nothing(*_):
                pass

            def split_high(w):
                act.wait_ge(s_wff[w], 16)
                a.activation(wff[:, :, 2 * w, :], stage[:, w, :].rearrange("p (e n) -> p e n", e=E), ACT.Copy,
                             scale=WSCALE).then_inc(s_wh, 1)

            act.wait_ge(s_wcp, 1)
            a.activation(wc[:], bank[0][:, 0:D], ACT.Copy).then_inc(s_wcs, 1)
            a.activation(cb[:], bank[0][0:1, D:2 * D], ACT.Copy).then_inc(s_wcs, 1)
            for k in range(PIECES_A):
                a_piece(0, k)
            split_high(0)
            split_high(1)
            layer_pass(a_piece, r_piece, x_step, nothing, 0)

            def front(b, j):
                slot = b % 3
                if j == 3:
                    evac_z(z_attn(b))
                elif j in (5, 8):
                    i, bias = (0, bq_s) if j == 5 else (1, bk_s)
                    act.wait_ge(s_qk, 2 * b + i + 1)
                    wait(act, s_dump, 64 * b)
                    a.activation(hi[:, i, :], bank[1][:, :], ACT.Identity, bias=bias[:, 0:1]).then_inc(s_hi, 1)
                elif j == 10:
                    act.wait_ge(s_vm, b + 1)
                    wait(act, s_pv, UNITS * (b - 2))
                    dst = vp[:, slot, :, 0:NH * VW].rearrange("p t (h j) -> p t h j", j=VW)
                    for t in range(TPB):
                        ins = a.activation(dst[:, t, :, 0:DK], bank[1][:, P * t:P * t + P].rearrange("p (h j) -> p h j", j=DK), ACT.Copy)
                    ins.then_inc(s_v, 1)
                elif j == 12:
                    act.wait_ge(s_vs, 2 * b + 1)
                    a.activation(vrow[:], bank[1][0:1, 0:D], ACT.Copy, scale=ATTN_EPS).then_inc(s_vsr, 1)
                elif j == 13:
                    act.wait_ge(s_vs, 2 * b + 2)
                    a.activation(vsum[:, slot, :], bank[1][:, 0:1], ACT.Copy).then_inc(s_vsr, 1)

            def exps(b, j):
                kt = j % TPB
                w = 256 if kt < TPB - 1 else 128
                i = UNITS * b + j
                act.wait_ge(s_st, i + 1)
                wait(act, s_pv, i - 2)
                src = stbank[:].rearrange("p a n -> p (a n)")[:, 1024 * (j % 2):1024 * (j % 2) + 4 * w]
                a.activation(pT[:, i % 3, 0:4 * w], src, ACT.Exp, scale=SCALE).then_inc(s_e, 1)

            def u_copy(b, s):
                act.wait_ge(s_pv, UNITS * b + TPB * (s + 1))
                wait(act, s_ut, TPB * b)
                a.activation(uT[:, s, :], bank[0][:, :], ACT.Copy).then_inc(s_u, 1)

            def ctx_copy(b):
                act.wait_ge(s_cxp, b + 1)
                a.activation(cT, bank[0][:, :], ACT.Identity, bias=vsum[:, b % 3, :]).then_inc(s_ct, 1)

            for b in range(2):
                for j in range(UNITS):
                    front(b, j)
            for b in range(B):
                act.wait_ge(s_mtp, b + 1)
                wait(act, s_md, 16 * b)
                a.activation(mT[:], bank[1][0:NH, :], ACT.Copy, scale=-1.0).then_inc(s_mt, 1)
                if b:
                    ctx_copy(b - 1)
                for j in range(UNITS):
                    exps(b, j)
                    if j and j % TPB == 1:
                        if j > 1:
                            u_copy(b, j // TPB - 1)
                    if b + 2 < B:
                        front(b + 2, j)
                u_copy(b, SETS - 1)
            ctx_copy(B - 1)
            layer_pass(nothing, r_piece, x_step, nothing, 1)

        @block.tensor
        def _(pe):
            mm = pe.matmul
            pe.wait_ge(s_const, N_CONST)
            pe.wait_ge(s_w, 16 * N_W)
            mm(bank[0][:, 0:D], wa_s[:], tri[:], start=True, stop=True)
            mm(bank[0][0:1, D:2 * D], ba_s[:], tri[:], start=True, stop=True).then_inc(s_wcp, 1)
            pe.wait_ge(s_wcs, 2)

            def transpose_z(n, dst):
                pe.wait_ge(s_z, n + 1)
                wait(pe, s_zt, n)
                for t in range(TPB):
                    ins = pe.transpose(dst[:, P * t:P * t + P], zr[:, n % 2, t, :], ident[:])
                ins.then_inc(s_zp, 1)

            def a_piece(c, k):
                if 6 <= k < 6 + BPC:
                    b = BPC * c + k - 6
                    n = z_linear(b)
                    transpose_z(n, bank[0])
                    pe.wait_ge(s_zt, n + 1)
                    wait(pe, s_aa, b)
                    if c and k == 6:
                        pe.wait_ge(s_idx, 1)
                    for t in range(TPB):
                        o = bank[1][:, P * t:P * t + P]
                        mm(o, zT[:, n % 2, P * t:P * t + P], wc[:], start=True, stop=False)
                        ins = mm(o, ones_row[:], cb[:], start=False, stop=True)
                    ins.then_inc(s_am, 1)
                    pe.sem_inc(s_ztf, 1)

            def r_piece(cc, k):
                if 6 <= k < 6 + BPC:
                    transpose_z(z_router(cc, k - 6), bank[0])
                if 7 <= k < 7 + BPC:
                    i = k - 7
                    n = z_router(cc, i)
                    pe.wait_ge(s_zt, n + 1)
                    if i == 0:
                        pe.wait_ge(s_aa, BPC * min(cc + 1, CHUNKS))
                        wait(pe, s_idx, cc)
                    for t in range(TPB):
                        ins = mm(LG[:, TPB * i + t, :], zT[:, n % 2, P * t:P * t + P], rw_s[:], start=True, stop=True)
                    if i == BPC - 1:
                        ins.then_inc(s_lg, 1)
                    pe.sem_inc(s_ztf, 1)
                elif k == 13:
                    pe.wait_ge(s_c16, cc + 1)
                    mm(RK, before16[:], c16[:], start=True, stop=False, skip_group_check=True)
                    for t in range(CT - 1):
                        n = CT - 1 - t
                        mm(RK[:, t + 1:CT, :], ones16[:], c16[:, t:t + 1, :].to_broadcast([P, n, E]), start=False,
                           stop=(t == CT - 2), skip_group_check=True)
                    for t in range(CT):
                        ins = mm(CN, ones16[:], c16[:, t, :], start=(t == 0), stop=(t == CT - 1))
                    ins.then_inc(s_cn, 1)
                elif 17 <= k <= 20:
                    pe.wait_ge(s_oh, 4 * cc + k - 16)
                    for t in range(TPB * (k - 17), TPB * (k - 17) + TPB):
                        for i in range(2):
                            ins = mm(IX, ohl[:, i, t, :], oht[:, i, t, :], start=(t == 0 and i == 0),
                                     stop=(t == CT - 1 and i == 1))
                    if k == 20:
                        ins.then_inc(s_ixp, 1)

            def x_step(cc, s):
                if s == 0:
                    pe.wait_ge(s_wl, 2)
                    pe.wait_ge(s_idx, cc + 1)
                if s < SLOT_TILES:
                    i = tile_of(cc, s)
                    pe.wait_ge(s_g[i % G], 16 * (i // G + 1))
                    wait(pe, s_xt, i - 1)
                    for a2 in range(2):
                        ins = pe.transpose(xbank[i % 2][:, P * a2:P * a2 + P], xg[:, i % G, a2, :], ident16[:])
                    ins.then_inc(s_xp, 1)
                if s % LOADS == 0 and s < SLOT_TILES:
                    n = min(LOADS, SLOT_TILES - s)
                    _, ids = nc.values_load_multi_w_load_instructions(
                        eid[0:1, cc % 2, s:s + n], [mybir.EngineType.PE], min_val=0, max_val=E - 1,
                        skip_runtime_bounds_check_because="a count of thresholds passed, cut off at E - 1")
                    for k in range(n):
                        experts[s + k] = wff[:, bass.ds(ids[k], 1), :, :]
                if 0 <= s - 2 < SLOT_TILES:
                    i = tile_of(cc, s - 2)
                    pe.wait_ge(s_xt, i + 1)
                    wait(pe, s_gh, i - 1)
                    xh, xl = xT[:, i % 3, 0:P], xT[:, i % 3, P:2 * P]
                    w = experts[s - 2]
                    for f in range(FC):
                        o = hbank[i % 2][:, P * f:P * f + P]
                        wh, wl = w[:, 0, 0, P * f:P * f + P], w[:, 0, 1, P * f:P * f + P]
                        mm(o, wh, xh, start=True, stop=False)
                        mm(o, wh, xl, start=False, stop=False)
                        ins = mm(o, wl, xh, start=False, stop=True)
                    ins.then_inc(s_h, 1)
                if 0 <= s - 4 < SLOT_TILES:
                    i = tile_of(cc, s - 4)
                    pe.wait_ge(s_gl, i + 1)
                    wait(pe, s_yc, i - 1)
                    o = ybank[i % 2]
                    w = experts[s - 4]
                    for f in range(FC):
                        whl = w[:, 0, 2:4, P * f:P * f + P]
                        mm(o, gh[:, i % 3, P * f:P * f + P], whl, start=(f == 0), stop=False, skip_group_check=True)
                        ins = mm(o[:, 0:P], gl[:, i % 3, P * f:P * f + P], whl[:, 0, :], start=False, stop=(f == FC - 1),
                                 skip_group_check=True)
                    ins.then_inc(s_y, 1)

            experts = {}

            def nothing(*_):
                pass

            for k in range(PIECES_A):
                a_piece(0, k)
            layer_pass(a_piece, r_piece, x_step, nothing, 0)
            pe.wait_ge(s_yc, tile_of(CHUNKS, 0))

            def front(b, j):
                n = z_attn(b)
                slot = b % 3
                if j == 3:
                    wait(pe, s_oa, b - 2)
                    wait(pe, s_vsr, 2 * b)
                    transpose_z(n, bank[1])
                elif j == 5:
                    pe.wait_ge(s_zt, n + 1)
                    mm(bank[1][:, :], wq_s[:], zT[:, n % 2, :], start=True, stop=True).then_inc(s_qk, 1)
                elif j == 8:
                    pe.wait_ge(s_lo, 2 * b + 1)
                    mm(bank[1][:, :], wk_s[:], zT[:, n % 2, :], start=True, stop=True).then_inc(s_qk, 1)
                elif j == 10:
                    pe.wait_ge(s_lo, 2 * b + 2)
                    for t in range(TPB):
                        o = bank[1][:, P * t:P * t + P]
                        mm(o, zT[:, n % 2, P * t:P * t + P], wv_s[:], start=True, stop=False)
                        ins = mm(o, ones_row[:], bv_s[:], start=False, stop=True)
                    ins.then_inc(s_vm, 1)
                    pe.sem_inc(s_ztf, 1)
                elif j == 12:
                    pe.wait_ge(s_v, b + 1)
                    for t in range(TPB):
                        vt = vp[:, slot, t, 0:NH * VW].rearrange("p (h j) -> p h j", j=VW)[:, :, 0:DK]
                        ins = mm(bank[1][0:1, 0:D], ones_col[:], vt, start=(t == 0), stop=(t == TPB - 1))
                    ins.then_inc(s_vs, 1)
                elif j == 13:
                    pe.wait_ge(s_vsr, 2 * b + 1)
                    mm(bank[1][:, 0:1], vrow[:], ones_row[0:1, 0:1], start=True, stop=True).then_inc(s_vs, 1)

            def scores(b, j):
                s, qt = j // TPB, j % TPB
                slot = b % 3
                if j == 0:
                    pe.wait_ge(s_stk[b % 2], 16 * 24 * (b // 2 + 1))
                    wait(pe, s_cx, TPB * (b - 1))
                wait(pe, s_red, UNITS * b + j)
                w = 256 if qt else 128
                k0 = P * (qt - 1) if qt else 0
                bank_ = sbank[:].rearrange("p a n -> p (a n)")
                for g in range(4):
                    ins = mm(bank_[:, w * g:w * g + w], qz[0:P - 1, slot, g * SETS + s, P * qt:P * qt + P],
                             kst[0:P - 1, slot, s, k0:k0 + w], start=True, stop=True)
                ins.then_inc(s_s, 1)

            def scores_t(b, j):
                s, kt = j // TPB, j % TPB
                slot = b % 3
                if j == 0:
                    pe.wait_ge(s_mr, 16 * (b + 1))
                wait(pe, s_e, UNITS * b + j - 1)
                w = 256 if kt < TPB - 1 else 128
                bank_ = stbank[:].rearrange("p a n -> p (a n)")[:, 1024 * (j % 2):1024 * (j % 2) + 1024]
                for g in range(4):
                    ins = mm(bank_[:, w * g:w * g + w], kst[:, slot, s, P * kt:P * kt + P],
                             qz[:, slot, g * SETS + s, P * kt:P * kt + w], start=True, stop=True)
                ins.then_inc(s_st, 1)

            def pv(b, j):
                s, kt = j // TPB, j % TPB
                w = 256 if kt < TPB - 1 else 128
                i = UNITS * b + j
                pe.wait_ge(s_pm, i + 1)
                if kt == 0:
                    wait(pe, s_u, SETS * b + s)
                    if s == 0:
                        wait(pe, s_ct, b)
                for g in range(4):
                    h = SETS * s + g
                    ins = mm(bank[0][32 * g:32 * g + 32, P * kt:P * kt + w], vp[:, b % 3, kt, VW * h:VW * h + 32],
                             pT[:, i % 3, w * g:w * g + w], start=(kt == 0), stop=(kt == TPB - 1),
                             tile_position=(0, 32 * g), skip_group_check=True)
                ins.then_inc(s_pv, 1)

            def max_rows(b):
                pe.wait_ge(s_red, UNITS * (b + 1))
                pe.wait_ge(s_vsr, 2 * min(b + 2, B))
                for t in range(TPB):
                    ins = pe.transpose(bank[1][0:NH, P * t:P * t + P], mx[:, t, :], ident[:])
                ins.then_inc(s_mtp, 1)

            def back(b):
                pe.wait_ge(s_u, SETS * (b + 1))
                for qt in range(TPB):
                    if qt >= 2:
                        pe.wait_ge(s_cx, TPB * b + qt - 1)
                    for s in range(SETS):
                        ins = pe.transpose(sbank[:, qt % 2, P * s:P * s + P], uT[:, s, P * qt:P * qt + P], ident[:])
                    ins.then_inc(s_ut, 1)
                for qt in range(TPB):
                    pe.wait_ge(s_cx, TPB * b + qt + 1)
                    ins = pe.transpose(bank[0][:, P * qt:P * qt + P], cx[:, qt, :], ident[:])
                ins.then_inc(s_cxp, 1)
                pe.wait_ge(s_ct, b + 1)
                pe.wait_ge(s_mt, min(b + 2, B))
                for t in range(TPB):
                    o = bank[1][:, P * t:P * t + P]
                    mm(o, cT[:, P * t:P * t + P], wo_s[:], start=True, stop=False)
                    ins = mm(o, ones_row[:], bo_s[:], start=False, stop=True)
                ins.then_inc(s_o, 1)

            for b in range(2):
                for j in range(UNITS):
                    front(b, j)
            for j in range(UNITS):
                scores(0, j)
            for b in range(B):
                max_rows(b)
                if b:
                    back(b - 1)
                for j in range(UNITS + 1):
                    if j < UNITS:
                        scores_t(b, j)
                        if b + 2 < B:
                            front(b + 2, j)
                        if b + 1 < B:
                            scores(b + 1, j)
                    if j:
                        pv(b, j - 1)
            back(B - 1)
            pe.wait_ge(s_oa, B)
            layer_pass(nothing, r_piece, x_step, nothing, 1)


def head_order():
    return [DK * (SETS * s + g) + j for g in range(4) for s in range(SETS) for j in range(DK)]


def kernel(L0_attn_a_x, L0_attn_a_W, L0_attn_a_bias, L0_attn_b_Wq, L0_attn_b_bq, L0_attn_b_Wk, L0_attn_b_bk,
           L0_attn_b_Wv, L0_attn_b_bv, L0_attn_b_Wo, L0_attn_b_bo, L0_ffn_gamma, L0_ffn_beta, L0_ffn_router_w,
           L0_ffn_W1, L0_ffn_W2):
    import numpy as np
    import concourse.bacc as bacc
    from concourse.bass_utils import run_bass_kernel_spmd

    order = head_order()
    layout = {
        "x": L0_attn_a_x, "wa": L0_attn_a_W, "ba": np.reshape(L0_attn_a_bias, (D, 1)),
        "wq": np.transpose(L0_attn_b_Wq)[:, order], "wk": np.transpose(L0_attn_b_Wk)[:, order],
        "wv": np.transpose(L0_attn_b_Wv), "wo": np.transpose(L0_attn_b_Wo),
        "bq": np.reshape(np.asarray(L0_attn_b_bq)[order], (D, 1)), "bk": np.reshape(np.asarray(L0_attn_b_bk)[order], (D, 1)),
        "bv": np.reshape(L0_attn_b_bv, (1, D)), "bo": np.reshape(L0_attn_b_bo, (1, D)),
        "gamma": np.reshape(L0_ffn_gamma, (D, 1)), "beta": np.reshape(L0_ffn_beta, (D, 1)),
        "rw": np.transpose(L0_ffn_router_w), "w1": L0_ffn_W1, "w2": L0_ffn_W2,
    }
    nc = bacc.Bacc("TRN2", target_bir_lowering=False, num_devices=1)
    arrays, args = {}, []
    for name, a in layout.items():
        a = np.ascontiguousarray(a)
        arrays[f"in_{name}"] = a
        args.append(nc.dram_tensor(f"in_{name}", a.shape, mybir.dt.from_np(a.dtype), kind="ExternalInput").ap())
    args.append(nc.dram_tensor("out", (B, SEQ, D), F32, kind="ExternalOutput").ap())
    build(nc, *args)
    r = run_bass_kernel_spmd(nc, [arrays], core_ids=[0])
    return r.results[0]["out"]
```

```python
from contextlib import ExitStack

import concourse.bass as bass
from concourse import mybir

F32 = mybir.dt.float32
F16 = mybir.dt.float16
I32 = mybir.dt.int32
U32 = mybir.dt.uint32
ALU = mybir.AluOpType
ACT = mybir.ActivationFunctionType
AX = mybir.AxisListType

P = 128
D = 128
B = 8
SEQ = 512
TPB = SEQ // P
NT = B * TPB
E = 8
H = 4 * D
FC = H // P
NH = 16
DK = D // NH
SETS = 4
EPS = 1e-5
TEMP = 1.5
SCALE = 1.0 / float(DK) ** 0.5
MASKED = -60000.0
ATTN_EPS = 1e-9
VW = DK + 1
VROW = NH * VW + 32
UNITS = SETS * TPB

BPC = 4
CT = BPC * TPB
CHUNK = CT * P
CHUNKS = B // BPC
SLOT_TILES = (2 * CHUNK + E * (P - 1)) // P
WSCALE = 64.0
G = 4
AHEAD = G - 1
ZERO_AT, ZEROS = 24, 12
GATHERS = 2 * TPB
BACK_AT = 4
LOAD_EVERY = 6
FRONT_AT = 14
FRONT_STEPS = 14
MAX_SPLIT = 3 * TPB
FRONT_EARLY = 4
MAX_AT = 12
LOADS = 4
A_BEFORE_R = 4
STEPS_R = 18


def build(nc, x, wa, ba, wq, wk, wv, wo, bq, bk, bv, bo, gamma, beta, rw, w1, w2, out):
    x_t = x.rearrange("b (t p) d -> p (b t) d", p=P)
    out_t = out.rearrange("b (t p) d -> p (b t) d", p=P)
    dumps = nc.dram_tensor("dumps", [2, 4, P, SEQ], F16).ap()
    mdump = nc.dram_tensor("mdump", [2, NH, SEQ], F16).ap()
    table = [nc.dram_tensor(f"table{i}", [CHUNK, 2 * D], F16).ap() for i in range(2)]
    yslot = [nc.dram_tensor(f"yslot{i}", [SLOT_TILES * P, D], F32).ap() for i in range(2)]
    ytab = [nc.dram_tensor(f"ytab{i}", [(2 * CHUNK) + SLOT_TILES * P, D], F32).ap() for i in range(2)]

    with ExitStack() as ctx:
        def sb(n, s, d=F32):
            return ctx.enter_context(nc.sbuf_tensor(n, s, d))

        def ps(n, s, d=F32):
            return ctx.enter_context(nc.psum_tensor(n, s, d))

        def sem(n):
            return ctx.enter_context(nc.semaphore(n))

        def wait(eng, s, v):
            if v > 0:
                eng.wait_ge(s, v)

        xs = sb("xs", [P, NT, D])
        wa_s = sb("wa_s", [P, D]); wc = sb("wc", [P, D]); cb = sb("cb", [1, D]); ba_s = sb("ba_s", [P, 1])
        wq_s = sb("wq_s", [P, D]); wk_s = sb("wk_s", [P, D]); wv_s = sb("wv_s", [P, D]); wo_s = sb("wo_s", [P, D])
        bq_s = sb("bq_s", [P, 1]); bk_s = sb("bk_s", [P, 1]); bv_s = sb("bv_s", [1, D]); bo_s = sb("bo_s", [1, D])
        ga_s = sb("ga_s", [P, 1]); be_s = sb("be_s", [P, 1]); rw_s = sb("rw_s", [P, E])
        ga_row = sb("ga_row", [P, D]); be_row = sb("be_row", [P, D])
        wff = sb("wff", [P, E, 4, H], F16)
        ident = sb("ident", [P, P]); ident16 = sb("ident16", [P, P], F16)
        tri = sb("tri", [P, P]); ones_row = sb("ones_row", [1, P]); ones_col = sb("ones_col", [P, 1])
        before16 = sb("before16", [P, P], F16); ones16 = sb("ones16", [P, P], F16)
        lane16 = sb("lane16", [P, P], F16); tile16 = sb("tile16", [P, SLOT_TILES], F16); token_id = sb("token_id", [P, 2, CT]); pad_row = sb("pad_row", [P, SLOT_TILES])
        steps = sb("steps", [P, E, CT]); upto = sb("upto", [P, E, E]); tiles3 = sb("tiles3", [1, SLOT_TILES, E])
        prefer = sb("prefer", [P, CT, E])
        mband = sb("mband", [P, 256], F16); mlower = sb("mlower", [P, P], F16)
        mhalf = sb("mhalf", [P, 2, CT])
        st = sb("st", [P, CT, 6]); mv = sb("mv", [P, CT, 2]); ve = sb("ve", [P, 2, CT]); r0 = sb("r0", [P, 2, CT])
        newt = sb("newt", [P, 2, CT]); rr = sb("rr", [P, 2, CT]); r1p = sb("r1p", [P, CT]); nmr = sb("nmr", [P, CT])
        zr = sb("zr", [P, 2, TPB, D]); zT = sb("zT", [P, 2, SEQ])
        lg = sb("lg", [P, CT, E]); pr = sb("pr", [P, CT, E]); key = sb("key", [P, CT, E]); oh = sb("oh", [P, 2, CT, E])
        lg2 = sb("lg2", [P, CT, E]); rm = sb("rm", [P, 4, CT]); c16 = sb("c16", [P, CT, E], F16)
        wk2 = sb("wk2", [P, 2, 2, CT]); pwork = sb("pwork", [P, 2, CT, E])
        cnt = sb("cnt", [P, E]); ge3 = sb("ge3", [P, E, CT]); te = sb("te", [P, E]); en = sb("en", [P, E]); off = sb("off", [P, E])
        pos = sb("pos", [P, 2, CT])
        posi = sb("posi", [P, 2, 2, CT], U32); lani = sb("lani", [P, 2, CT], I32); tili = sb("tili", [P, 2, CT], I32)
        lanf = sb("lanf", [P, 2, CT]); tilf = sb("tilf", [P, 2, CT])
        ohl = sb("ohl", [P, 2, CT, P], F16); oht = sb("oht", [P, 2, CT, SLOT_TILES], F16)
        idx = sb("idx", [P, 2, SLOT_TILES], U32); sidx = sb("sidx", [P, 2, SLOT_TILES], U32)
        eg3 = sb("eg3", [1, SLOT_TILES, E]); egf = sb("egf", [1, SLOT_TILES]); eid = sb("eid", [1, 2, SLOT_TILES], I32)
        xnb = sb("xnb", [P, 2, TPB, D]); tb = sb("tb", [P, 2, TPB, 2, D], F16)
        xg = sb("xg", [P, G, 2, D], F16); xT = sb("xT", [P, 3, 2 * P], F16)
        g32 = sb("g32", [P, 3, H]); gh = sb("gh", [P, 3, H], F16); gl = sb("gl", [P, 3, H], F16)
        ysb = sb("ysb", [P, G, D]); cg = sb("cg", [P, 2, TPB, 2, D])
        hi = sb("hi", [P, 2, SEQ], F16); lo = sb("lo", [P, 2, SEQ], F16)
        qz = sb("qz", [P, 3, NH, SEQ], F16); kst = sb("kst", [P, 3, SETS, SEQ], F16)
        vp = sb("vp", [P, 3, TPB, VROW]); vsum = sb("vsum", [P, 3, 1]); vrow = sb("vrow", [1, D])
        mx = sb("mx", [P, TPB, NH]); mT = sb("mT", [NH, SEQ], F16)
        pT = sb("pT", [P, 3, 4 * 256])
        posb = key
        uT = ohl[:].rearrange("p k t n -> p (k t n)").bitcast(F32).rearrange("p (s n) -> p s n", s=SETS)
        cx = g32[:, 0, :].rearrange("p (t d) -> p t d", t=TPB)
        cT = g32[:, 1, :]
        rden = lg[:, 0:TPB * NH // E, :].rearrange("p (t a) e -> p t (a e)", t=TPB)
        stage = qz[:].rearrange("p u h n -> p (u h n)")[:, 0:4 * E * H].bitcast(F32).rearrange("p (w n) -> p w n", w=2)

        bank = [ps(f"bank{i}", [P, 512]) for i in range(2)]
        sbank = ps("sbank", [P, 2, 512])
        stbank = ps("stbank", [P, 4, 512])
        RK = bank[1][:, CT * E:2 * CT * E].rearrange("p (t e) -> p t e", e=E)
        CN = bank[1][:, 2 * CT * E:2 * CT * E + E]
        IX = bank[1][:, 2 * CT * E + E:2 * CT * E + E + SLOT_TILES]
        xbank = [sbank[:, i, 0:P].bitcast(F16) for i in range(2)]
        hbank = [stbank[:, i, :] for i in range(2)]
        ybank = stbank[:, 2, 0:2 * D]

        s_x = [sem(f"x{b}_loaded") for b in range(B)]; s_wa = sem("linear_loaded"); s_w = sem("weights_loaded")
        s_wff = [sem(f"w{i}_staged") for i in range(2)]; s_wh = sem("weights_high"); s_wl = sem("weights_low")
        s_const = sem("constants_made"); s_chain = sem("pool_chain"); s_wcp = sem("wc_psum"); s_wcs = sem("wc_ready")
        s_ve = sem("variance_ready"); s_r0 = sem("rsqrt_guess")
        s_res = sem("residual_scaled")
        s_z = sem("z_ready"); s_zp = sem("z_transposed"); s_zt = sem("zt_ready"); s_ztf = sem("zt_used")
        s_am = sem("linear_psum"); s_aa = sem("linear_added")
        s_xn = sem("xn_ready"); s_xh = sem("xn_high"); s_tb = sem("table_rows_ready")
        s_tbd = [sem(f"table_rows_stored{i}") for i in range(2)]
        s_lg = sem("logits_psum"); s_lc = sem("logits_centred"); s_pe = sem("probs_exp")
        s_c16 = sem("choices_ready"); s_cn = sem("counts_psum"); s_oh = sem("slot_onehots"); s_ixp = sem("slots_psum")
        s_idx = sem("slot_indices_ready")
        s_g = [sem(f"gathered{i}") for i in range(G)]; s_xp = sem("x_transposed"); s_xt = sem("xt_ready")
        s_h = sem("h_psum"); s_gh = sem("g_ready"); s_gl = sem("g_low_ready"); s_y = sem("y_psum"); s_yc = sem("y_copied")
        s_ys = [sem(f"y_stored{i}") for i in range(G)]; s_sc = [sem(f"y_scattered{i}") for i in range(G)]
        s_cg = [sem(f"y_gathered{i}") for i in range(2)]; s_cl = [sem(f"y_loaded{i}") for i in range(2)]; s_cd = sem("combined")
        s_qk = sem("qk_psum"); s_hi = sem("hi_ready"); s_lo = sem("lo_ready"); s_vm = sem("v_psum"); s_v = sem("v_ready")
        s_vs = sem("vsum_psum"); s_vsr = sem("vsum_ready")
        s_dump = sem("qk_dumped"); s_stk = [sem(f"stacks_loaded{i}") for i in range(2)]; s_zero = sem("stacks_zeroed")
        s_s = sem("s_psum"); s_red = sem("s_reduced"); s_mtp = sem("max_transposed"); s_mt = sem("max_ready")
        s_md = sem("max_dumped"); s_mr = [sem(f"max_rows_loaded{i}") for i in range(2)]
        s_st = sem("st_psum"); s_e = sem("exp_ready"); s_pm = sem("p_masked"); s_pmc = sem("p_mask_half")
        s_pv = sem("pv_done"); s_u = sem("u_copied")
        s_ut = sem("u_transposed"); s_cx = sem("ctx_ready"); s_cxp = sem("ctx_transposed"); s_ct = sem("ct_ready")
        s_o = sem("o_psum"); s_oa = sem("o_added"); s_out = sem("stored")

        block = ctx.enter_context(nc.Block())
        N_W = 13
        N_CONST = 1

        def z_linear(b):
            return b if b < BPC else 2 * BPC + (b - BPC)

        def z_router(cc, i):
            return (BPC, 3 * BPC, 6 * BPC, 7 * BPC)[cc] + i

        def z_attn(b):
            return 4 * BPC + b

        def logits_bank(cc):
            return (sbank[:, 0, 0:CT * E] if cc == CHUNKS else stbank[:, 3, 0:CT * E]).rearrange("p (t e) -> p t e", e=E)

        def routed(n):
            return sum(z_router(cc, i) <= n for cc in range(2 * CHUNKS) for i in range(BPC))

        def z_bank(n):
            return bank[1] if z_attn(0) <= n < z_attn(B) else sbank[:, 1, :] if n // BPC == z_router(CHUNKS, 0) // BPC else bank[0]

        XSTEPS = SLOT_TILES + 5

        def tile_of(cc, t):
            return SLOT_TILES * cc + t

        def scattered(slot, end):
            return (end - 1 - slot) // G - (tile_of(CHUNKS, 0) - 1 - slot) // G

        def gathered_back_at(s):
            return s - BACK_AT if 0 <= s - BACK_AT < BPC * GATHERS else None

        def loaded_back_at(s):
            b = (s - BACK_AT) // LOAD_EVERY
            return b if s >= BACK_AT and (s - BACK_AT) % LOAD_EVERY == 0 and b < BPC else None

        def combined_at(layer, s):
            if layer:
                return loaded_back_at(s - 3)
            b = s - BACK_AT - GATHERS - 1
            return b // GATHERS if b >= 0 and b % GATHERS == 0 and b // GATHERS < BPC else None

        def prepared_at(s):
            return ((s - FRONT_AT) // FRONT_STEPS, (s - FRONT_AT) % FRONT_STEPS) if 0 <= s - FRONT_AT < 2 * FRONT_STEPS else None

        def first_router(a_step, r_step):
            for k in range(A_BEFORE_R + STEPS_R):
                a_step(0, k)
                r_step(0, k - A_BEFORE_R)

        def layer_pass(a_step, r_step, x_step, beside, layer):
            c0 = CHUNKS * layer
            for s in range(XSTEPS):
                x_step(c0, s)
                if layer == 0:
                    a_step(1, s)
                    r_step(c0 + 1, s - A_BEFORE_R)
                else:
                    r_step(c0 + 1, s)
            for s in range(XSTEPS):
                x_step(c0 + 1, s)
                beside(layer, s)

        def front_in_attention(front, b, j):
            if b + 2 < B:
                front(b + 2, j + FRONT_EARLY)
            if b + 3 < B and j >= UNITS - FRONT_EARLY:
                front(b + 3, j - (UNITS - FRONT_EARLY))

        def router_in_attention(r_step, b, j):
            k = UNITS * (b - (B - 1)) + j + 2
            if 0 <= k:
                r_step(CHUNKS, k)

        @block.sync
        def _(sp):
            def load_x(b):
                sp.dma_start(xs[:, TPB * b:TPB * b + TPB, :], x_t[:, TPB * b:TPB * b + TPB, :]).then_inc(s_x[b], 16)
            load_x(0)
            for d, s in ((wa_s, wa), (ba_s, ba)):
                sp.dma_start(d[:], s).then_inc(s_wa, 16)
            for b in range(1, BPC):
                load_x(b)
            for d, s in ((ga_s, gamma), (be_s, beta), (rw_s, rw), (wq_s, wq), (wk_s, wk), (wv_s, wv),
                         (wo_s, wo), (bq_s, bq), (bk_s, bk), (bv_s, bv), (bo_s, bo)):
                sp.dma_start(d[:], s).then_inc(s_w, 16)
            for d, s in ((ga_row, gamma), (be_row, beta)):
                sp.dma_start(d[:], s.rearrange("d a -> a d").to_broadcast([P, D])).then_inc(s_w, 16)
            for w, src in ((0, w1.rearrange("e d f -> d e f")), (1, w2.rearrange("e (c p) d -> p (e c) d", p=P))):
                sp.dma_start(stage[:, w, :].rearrange("p (a n) -> p a n", n=src.shape[2]), src).then_inc(s_wff[w], 16)
            for b in range(BPC, B):
                load_x(b)

            def nothing(*_):
                pass

            def r_step(cc, k):
                i = k - 5
                if 0 <= i < BPC:
                    if i == 0:
                        wait(sp, s_xp, SLOT_TILES * (cc - 1))
                    sp.wait_ge(s_tb, BPC * cc + i + 1)
                    sp.dma_start(table[cc % 2][SEQ * i:SEQ * (i + 1), :].rearrange("(t p) n -> p t n", p=P),
                                 tb[:, i % 2].rearrange("p t a d -> p t (a d)")).then_inc(s_tbd[i % 2], 16)

            def x_step(cc, s):
                t = s - 5
                if cc < CHUNKS and t >= 0:
                    i = tile_of(cc, t)
                    sp.wait_ge(s_yc, i + 1)
                    sp.dma_start(yslot[cc % 2][P * t:P * t + P, :], ysb[:, i % G, :]).then_inc(s_ys[i % G], 16)

            def load_back(b):
                cc = CHUNKS + b // BPC
                if b % BPC == 0:
                    last = tile_of(cc + 1, 0)
                    for i in range(G):
                        sp.wait_ge(s_sc[i], 16 * scattered(i, last))
                sp.wait_ge(s_ixp, CHUNKS + 1)
                sp.wait_ge(s_cd, B + b - 1)
                for k in range(2):
                    r = CHUNK * k + SEQ * (b % BPC)
                    sp.dma_start(cg[:, b % 2, :, k, :], ytab[cc % 2][r:r + SEQ, :].rearrange("(t p) d -> p t d", p=P)
                                 ).then_inc(s_cl[b % 2], 16)

            def store_out(b):
                sp.wait_ge(s_cd, B + b + 1)
                sp.dma_start(out_t[:, TPB * b:TPB * b + TPB, :], xs[:, TPB * b:TPB * b + TPB, :]).then_inc(s_out, 16)

            def load_stacks(b, k):
                par, slot = b % 2, b % 3
                if k < 2:
                    if k == 0:
                        wait(sp, s_s, 2 * UNITS * (b - 1))
                    sp.wait_ge(s_hi, 2 * b + k + 1)
                    sp.dma_start(dumps[par, 2 * k], hi[:, k, :]).then_inc(s_dump, 16)
                    sp.wait_ge(s_lo, 2 * b + k + 1)
                    sp.dma_start(dumps[par, 2 * k + 1], lo[:, k, :]).then_inc(s_dump, 16)
                    return
                if k == 2:
                    sp.wait_ge(s_dump, 64 * (b + 1))
                    sp.wait_ge(s_zero, ZEROS)
                    wait(sp, s_st, UNITS * (b - 2))
                for m in (2 * (k - 2), 2 * (k - 2) + 1):
                    i, g, c = m // 12, m // 3 % 4, m % 3
                    part = ((0, 0, 1), (0, 1, 0))[i][c]
                    src = dumps[par, 2 * i + part].rearrange("(g s j) n -> g j s n", g=4, s=SETS)[g]
                    r = 32 * g + DK * c
                    dst = (qz[r:r + DK, slot].rearrange("p (s g) n -> p s g n", g=4)[:, :, g, :] if i == 0 else kst[r:r + DK, slot, :, :])
                    sp.dma_start(dst, src).then_inc(s_stk[par], 16)

            def beside(layer, s):
                if layer == 1 and loaded_back_at(s) is not None:
                    load_back(loaded_back_at(s))
                if layer == 1 and combined_at(layer, s - 2) is not None:
                    store_out(combined_at(layer, s - 2))
                if layer == 0:
                    for b in range(2):
                        k = s - (FRONT_AT + FRONT_STEPS * b + 9)
                        if k == 0:
                            load_stacks(b, 0)
                        elif k == 3:
                            load_stacks(b, 1)
                        elif k > 3 and k - 2 < 14:
                            load_stacks(b, k - 2)

            first_router(nothing, r_step)
            layer_pass(nothing, r_step, x_step, beside, 0)
            for k in range(XSTEPS - (FRONT_AT + FRONT_STEPS + 9) - 2, 14):
                load_stacks(1, k)

            def max_rows(b, part):
                rows = slice(0, MAX_SPLIT) if part == 0 else slice(MAX_SPLIT, NH)
                sp.wait_ge(s_mt, 2 * b + part + 1)
                sp.dma_start(mdump[b % 2, rows], mT[0:rows.stop - rows.start]).then_inc(s_md, 16)
                sp.wait_ge(s_md, 16 * (2 * b + part + 1))
                sp.dma_start(qz[P - 1:P, b % 3, rows, :], mdump[b % 2, rows].rearrange("(a h) n -> a h n", a=1)
                             ).then_inc(s_mr[part], 16)

            max_rows(0, 0)
            max_rows(0, 1)
            for b in range(B):
                if b + 2 < B:
                    for k in range(14):
                        load_stacks(b + 2, k)
                if b + 1 < B:
                    max_rows(b + 1, 0)
                    max_rows(b + 1, 1)
            for k in range(STEPS_R):
                r_step(CHUNKS, k)
            layer_pass(nothing, r_step, x_step, beside, 1)
            load_back(BPC)
            for b in range(BPC, B):
                if b + 1 < B:
                    load_back(b + 1)
                store_out(b)
            sp.wait_ge(s_out, 16 * B)

        @block.gpsimd
        def _(pool):
            g = nc.gpsimd
            made_n = [0]

            def made(ins):
                made_n[0] += 1
                ins.then_inc(s_chain, 1)

            for t, v in ((ident, 0.0), (tri, 1.0), (ones_row, 1.0), (ones_col, 1.0), (before16, 1.0), (ones16, 1.0),
                         (upto, 1.0), (mhalf, -0.5)):
                made(g.memset(t[:], v))
            any_ = dict(allow_small_or_imprecise_dtypes=True)
            made(g.iota(lane16[:], pattern=[[1, P]], base=0, channel_multiplier=0, **any_))
            made(g.iota(tile16[:], pattern=[[1, SLOT_TILES]], base=0, channel_multiplier=0, **any_))
            made(g.iota(token_id[:, 0, :], pattern=[[P, CT]], base=1, channel_multiplier=1, **any_))
            made(g.iota(token_id[:, 1, :], pattern=[[-P, CT]], base=-1, channel_multiplier=-1, **any_))
            made(g.iota(pad_row[:], pattern=[[P, SLOT_TILES]], base=2 * CHUNK + 1, channel_multiplier=1, **any_))
            made(g.iota(steps[:], pattern=[[0, E], [P, CT]], base=0, channel_multiplier=0, **any_))
            made(g.iota(tiles3[:], pattern=[[1, SLOT_TILES], [0, E]], base=0, channel_multiplier=0, **any_))
            made(g.iota(prefer[:], pattern=[[0, CT], [-1, E]], base=E, channel_multiplier=0, **any_))
            pool.wait_ge(s_chain, made_n[0])
            made(g.affine_select(out=ident[:], in_=ident[:], compare_op=ALU.not_equal, fill=1.0, base=0,
                                 pattern=[[1, P]], channel_multiplier=-1))
            made(g.affine_select(out=tri[:], in_=tri[:], compare_op=ALU.is_ge, fill=0.0, base=0,
                                 pattern=[[1, P]], channel_multiplier=-1))
            made(g.affine_select(out=before16[:], in_=before16[:], compare_op=ALU.is_ge, fill=0.0, base=-1,
                                 pattern=[[1, P]], channel_multiplier=-1))
            made(g.affine_select(out=upto[:], in_=upto[:], compare_op=ALU.is_ge, fill=0.0, base=0,
                                 pattern=[[1, E], [-1, E]], channel_multiplier=0))
            pool.wait_ge(s_chain, made_n[0])
            g.tensor_copy(ident16[:], ident[:]).then_inc(s_const, 1)

            def pow_(n, col, both):
                pool.wait_ge(s_ve, n + 1)
                w, c = (slice(0, 1 + both), slice(col, col + TPB))
                g.tensor_tensor(r0[:, w, c], ve[:, w, c], mhalf[:, w, c], ALU.pow).then_inc(s_r0, 1)

            def a_step(c, k):
                if k < BPC:
                    pow_(z_linear(BPC * c + k), TPB * k, 0)
                if c == 0 and k == BPC - 1:
                    made(g.memset(kst[:], 0.0))
                    made(g.memset(vp[:], 1.0))
                    made(g.memset(mband[:], 0.0))
                    made(g.memset(mlower[:], 0.0))

            def r_step(cc, k):
                i = k - 2
                if 0 <= i < BPC:
                    if cc == 0 and i == 0:
                        pool.wait_ge(s_w, 16 * N_W)
                    n = z_router(cc, i)
                    pool.wait_ge(s_z, n + 1)
                    wait(pool, s_tb, BPC * cc + i - 1)
                    xn = xnb[:, i % 2]
                    made(g.tensor_tensor(xn, zr[:, n % 2], ga_row[:].unsqueeze(1).to_broadcast([P, TPB, D]), ALU.mult))
                    pool.wait_ge(s_chain, made_n[0])
                    g.tensor_tensor(xn, xn, be_row[:].unsqueeze(1).to_broadcast([P, TPB, D]), ALU.add).then_inc(s_xn, 1)
                if 0 <= k < BPC:
                    pow_(z_router(cc, k), TPB * k, 1)

            def x_step(cc, s):
                if cc == 0 and ZERO_AT <= s < ZERO_AT + ZEROS:
                    if s == ZERO_AT:
                        pool.wait_ge(s_wl, 2)
                        pool.wait_ge(s_wh, 2)
                    n = 3 * NH * SEQ // ZEROS
                    z = qz[:].rearrange("p u h n -> p (u h n)")[:, n * (s - ZERO_AT):n * (s - ZERO_AT + 1)]
                    g.memset(z.bitcast(F32), 0.0).then_inc(s_zero, 1)
                if s == 0:
                    pool.wait_ge(s_idx, cc + 1)
                    for i in range(2):
                        pool.wait_ge(s_tbd[i], 16 * 2 * (cc + 1))
                for t in range(AHEAD + 1) if s == 0 else (s + AHEAD,):
                    if t < SLOT_TILES:
                        i = tile_of(cc, t)
                        wait(pool, s_xp, i - G + 1)
                        g.indirect_dma_start(xg[:, i % G].rearrange("p a d -> p (a d)"), None, table[cc % 2],
                                             bass.IndirectOffsetOnAxis(ap=idx[:, cc % 2, t:t + 1], axis=0)).then_inc(s_g[i % G], 16)
                for t in (s - 6,) if s < XSTEPS - 1 else (s - 6, s - 5):
                    if cc >= CHUNKS and t >= 0:
                        i = tile_of(cc, t)
                        pool.wait_ge(s_yc, i + 1)
                        g.indirect_dma_start(ytab[cc % 2], bass.IndirectOffsetOnAxis(ap=sidx[:, cc % 2, t:t + 1], axis=0),
                                             ysb[:, i % G, :], None).then_inc(s_sc[i % G], 16)

            def gather_back(b, m):
                t, k = m // 2, m % 2
                cc = b // BPC
                if m == 0:
                    if b % BPC == 0:
                        last = tile_of(cc + 1, 0)
                        for i in range(G):
                            pool.wait_ge(s_ys[i], 16 * ((last - 1 - i) // G + 1))
                    wait(pool, s_cd, b - 1)
                at = (b % BPC) * TPB + t
                g.indirect_dma_start(cg[:, b % 2, t, k, :], None, yslot[cc % 2],
                                     bass.IndirectOffsetOnAxis(ap=posi[:, cc % 2, k, at:at + 1], axis=0)
                                     ).then_inc(s_cg[b % 2], 16)

            def front(b, j):
                if j == 2:
                    pow_(z_attn(b), 0, 0)

            def beside(layer, s):
                m = gathered_back_at(s)
                if layer == 0 and m is not None:
                    gather_back(m // GATHERS, m % GATHERS)
                if layer == 0 and prepared_at(s):
                    front(*prepared_at(s))

            def split_low(w):
                pool.wait_ge(s_wh, w + 1)
                g.tensor_tensor(wff[:, :, 2 * w + 1, :], stage[:, w, :].rearrange("p (e n) -> p e n", e=E),
                                wff[:, :, 2 * w, :], ALU.subtract).then_inc(s_wl, 1)

            first_router(a_step, r_step)
            pool.wait_ge(s_chain, made_n[0])
            made(g.affine_select(out=mband[:], in_=mband[:], compare_op=ALU.is_ge, fill=MASKED, base=0,
                                 pattern=[[1, 256]], channel_multiplier=-1))
            made(g.affine_select(out=mlower[:], in_=mlower[:], compare_op=ALU.is_ge, fill=MASKED, base=0,
                                 pattern=[[-1, P]], channel_multiplier=1))
            made(g.affine_select(out=kst[:], in_=kst[:], compare_op=ALU.not_equal, fill=1.0, base=-(P - 1),
                                 pattern=[[0, 3], [0, SETS], [0, SEQ]], channel_multiplier=1))
            pool.wait_ge(s_chain, made_n[0])
            made(g.affine_select(out=mband[:], in_=mband[:], compare_op=ALU.is_ge, fill=MASKED, base=P,
                                 pattern=[[-1, 256]], channel_multiplier=1))
            pool.wait_ge(s_chain, made_n[0])
            split_low(0)
            split_low(1)
            layer_pass(a_step, r_step, x_step, beside, 0)

            def mask(b, j):
                kt = j % TPB
                w = 256 if kt < TPB - 1 else 128
                i = UNITS * b + j
                pool.wait_ge(s_e, i + 1)
                p = pT[:, i % 3, 0:4 * w].rearrange("p (h q) -> p h q", q=w)
                ins = g.affine_select(out=p[:, :, 0:P], in_=p[:, :, 0:P], compare_op=ALU.is_ge, fill=0.0, base=0,
                                      pattern=[[0, 4], [1, P]], channel_multiplier=-1)
                if w == 256:
                    ins = g.affine_select(out=p[:, :, P:256], in_=p[:, :, P:256], compare_op=ALU.is_ge, fill=0.0, base=0,
                                          pattern=[[0, 4], [-1, P]], channel_multiplier=1)
                ins.then_inc(s_pm, 1)

            front(2, 2)
            for b in range(B):
                for j in range(UNITS):
                    mask(b, j)
                    if BPC <= b + 4 < B and j in (UNITS - 3, UNITS - 1):
                        gather_back(b + 4, (j - (UNITS - 3)) // 2)
                    if BPC <= b + 3 < B and j % 2 == 0 and j // 2 + 2 < GATHERS:
                        gather_back(b + 3, j // 2 + 2)
                    front_in_attention(front, b, j)
                    router_in_attention(r_step, b, j)
            layer_pass(a_step, r_step, x_step, beside, 1)

        @block.vector
        def _(dve):
            v = nc.vector

            def norm_begin(tile, col, both):
                for t in range(TPB):
                    v.bn_stats(st[:, col + t, :], xs[:, tile + t, :])
                dve.drain()
                for t in range(TPB):
                    v.bn_aggr(mv[:, col + t, :], st[:, col + t, :])
                dve.drain()
                var, c = mv[:, col:col + TPB, 1], slice(col, col + TPB)
                ins = v.tensor_scalar(ve[:, 0, c], var, EPS, None, ALU.add)
                if both:
                    ins = v.tensor_scalar(ve[:, 1, c], var, 1.0 + EPS, EPS * EPS, ALU.mult, ALU.add)
                ins.then_inc(s_ve, 1)

            def norm_end(n, col, both):
                dve.wait_ge(s_r0, n + 1)
                w, c = (slice(0, 1 + both), slice(col, col + TPB))
                v.tensor_tensor(newt[:, w, c], r0[:, w, c], r0[:, w, c], ALU.mult)
                dve.drain()
                v.tensor_tensor(newt[:, w, c], newt[:, w, c], ve[:, w, c], ALU.mult)
                dve.drain()
                v.tensor_scalar(newt[:, w, c], newt[:, w, c], -0.5, 1.5, ALU.mult, ALU.add)
                dve.drain()
                v.tensor_tensor(rr[:, w, c], r0[:, w, c], newt[:, w, c], ALU.mult)
                dve.drain()

            def normalise(n, tile, col, which):
                wait(dve, s_zp, n - 1)
                wait(dve, s_xn, routed(n - 2))
                for t in range(TPB):
                    ins = v.tensor_scalar(zr[:, n % 2, t, :], xs[:, tile + t, :], mv[:, col + t, 0:1],
                                          rr[:, which, col + t:col + t + 1], ALU.subtract, ALU.mult)
                ins.then_inc(s_z, 1)

            def flat(b):
                return xs[:, TPB * b:TPB * b + TPB, :].rearrange("p t d -> p (t d)")

            def a_step(c, k):
                i = k - A_BEFORE_R
                if 0 <= i < BPC:
                    b = BPC * c + i
                    dve.wait_ge(s_am, b + 1)
                    v.tensor_tensor(flat(b), flat(b), bank[1][:, :], ALU.add).then_inc(s_aa, 1)
                    dve.drain()
                if k < BPC:
                    b = BPC * c + k
                    dve.wait_ge(s_x[b], 16)
                    norm_begin(TPB * b, TPB * k, 0)
                if 0 <= k - 1 < BPC:
                    b = BPC * c + k - 1
                    norm_end(z_linear(b), TPB * (k - 1), 0)
                    normalise(z_linear(b), TPB * b, TPB * (k - 1), 0)

            def r_step(cc, k):
                c, cp = cc % CHUNKS, cc % 2
                ohl_ = cg[:].rearrange("p s t k d -> p (s t k d)").bitcast(F16).rearrange(
                    "p (k t n) -> p k t n", k=2, t=CT) if cc == CHUNKS else ohl

                def over_e(a):
                    return a.unsqueeze(2).to_broadcast([P, CT, E])

                if 0 <= k < BPC:
                    norm_begin(CT * c + TPB * k, TPB * k, 1)
                i = k - 4
                if 0 <= i < BPC:
                    dve.wait_ge(s_xh, BPC * cc + i + 1)
                    v.tensor_tensor(tb[:, i % 2, :, 1, :], xnb[:, i % 2], tb[:, i % 2, :, 0, :],
                                    ALU.subtract).then_inc(s_tb, 1)
                i = k - 1
                if 0 <= i < BPC:
                    n, cols = z_router(cc, i), slice(TPB * i, TPB * i + TPB)
                    norm_end(n, TPB * i, 1)
                    wait(dve, s_res, BPC * cc)
                    v.tensor_scalar(r1p[:, cols], rr[:, 0, cols], 1.0, None, ALU.add)
                    v.scalar_tensor_tensor(out=nmr[:, cols], in0=mv[:, cols, 0], scalar=-1.0, in1=rr[:, 0, cols],
                                           op0=ALU.mult, op1=ALU.mult)
                    normalise(n, CT * c + TPB * i, TPB * i, 1)
                elif k == 7:
                    dve.wait_ge(s_lg, cc + 1)
                    v.tensor_copy(lg[:], logits_bank(cc))
                    dve.drain()
                    v.tensor_reduce(rm[:, 0, :], lg[:], AX.X, ALU.max)
                    dve.drain()
                    v.tensor_tensor(lg[:], lg[:], over_e(rm[:, 0, :]), ALU.subtract).then_inc(s_lc, 1)
                    dve.drain()
                    v.scalar_tensor_tensor(out=key[:], in0=lg[:], scalar=0.0, in1=prefer[:], op0=ALU.is_equal, op1=ALU.mult)
                    dve.drain()
                    v.tensor_reduce(rm[:, 1, :], key[:], AX.X, ALU.max)
                    dve.drain()
                    v.tensor_tensor(oh[:, 0], key[:], over_e(rm[:, 1, :]), ALU.is_equal)
                    dve.drain()
                elif k == 8:
                    v.scalar_tensor_tensor(out=lg2[:], in0=oh[:, 0], scalar=-1e30, in1=lg[:], op0=ALU.mult, op1=ALU.add)
                    dve.drain()
                    v.tensor_reduce(rm[:, 2, :], lg2[:], AX.X, ALU.max)
                    dve.drain()
                    v.tensor_tensor(key[:], lg2[:], over_e(rm[:, 2, :]), ALU.is_equal)
                    dve.drain()
                    v.tensor_tensor(key[:], key[:], prefer[:], ALU.mult)
                    dve.drain()
                    v.tensor_reduce(rm[:, 1, :], key[:], AX.X, ALU.max)
                    dve.drain()
                    v.tensor_tensor(oh[:, 1], key[:], over_e(rm[:, 1, :]), ALU.is_equal)
                    dve.drain()
                    v.tensor_tensor(c16[:], oh[:, 0], oh[:, 1], ALU.add).then_inc(s_c16, 1)
                elif k == 9:
                    dve.wait_ge(s_pe, cc + 1)
                    v.tensor_reduce(rm[:, 3, :], pr[:], AX.X, ALU.add)
                    for i in range(2):
                        v.tensor_tensor(pwork[:, i], oh[:, i], pr[:], ALU.mult)
                    dve.drain()
                    v.reciprocal(rm[:, 3, :], rm[:, 3, :])
                    v.tensor_reduce(wk2[:, cp], pwork[:], AX.X, ALU.add)
                    dve.drain()
                    v.scalar_tensor_tensor(out=wk2[:, cp], in0=wk2[:, cp], scalar=1.0 / WSCALE,
                                           in1=rm[:, 3, :].unsqueeze(1).to_broadcast([P, 2, CT]), op0=ALU.mult, op1=ALU.mult)
                elif k == 10:
                    dve.wait_ge(s_cn, cc + 1)
                    v.tensor_copy(cnt[:], CN)
                    dve.drain()
                    v.tensor_tensor(ge3[:], cnt[:].unsqueeze(2).to_broadcast([P, E, CT]), steps[:], ALU.is_gt)
                    dve.drain()
                    v.tensor_reduce(te[:], ge3[:], AX.X, ALU.add)
                    dve.drain()
                    v.tensor_tensor(ge3[:, :, 0:E], te[:].unsqueeze(1).to_broadcast([P, E, E]), upto[:], ALU.mult)
                    dve.drain()
                    v.tensor_reduce(en[:], ge3[:, :, 0:E], AX.X, ALU.add)
                    dve.drain()
                    v.tensor_tensor(off[:], en[:], te[:], ALU.subtract)
                    dve.drain()
                    v.tensor_scalar(off[:], off[:], float(P), None, ALU.mult)
                    dve.drain()
                    v.tensor_tensor(posb[:], RK, off[:].unsqueeze(1).to_broadcast([P, CT, E]), ALU.add)
                    dve.drain()
                    for i in range(2):
                        v.tensor_tensor(pwork[:, i], oh[:, i], posb[:], ALU.mult)
                    dve.drain()
                    v.tensor_reduce(pos[:], pwork[:], AX.X, ALU.add)
                    dve.drain()
                elif k == 11:
                    pi = posi[:, cp]
                    v.tensor_copy(pi, pos[:])
                    dve.drain()
                    v.tensor_scalar(lani[:], pi.bitcast(I32), P - 1, None, ALU.bitwise_and)
                    v.tensor_scalar(tili[:], pi.bitcast(I32), P.bit_length() - 1, None, ALU.arith_shift_right)
                    v.tensor_tensor(eg3[:], tiles3[:], en[0:1, :].unsqueeze(1).to_broadcast([1, SLOT_TILES, E]), ALU.is_ge)
                    dve.drain()
                    v.tensor_copy(lanf[:], lani[:])
                    v.tensor_copy(tilf[:], tili[:])
                    v.tensor_reduce(egf[:], eg3[:], AX.X, ALU.add)
                    dve.drain()
                    v.tensor_scalar(eid[:, cp, :], egf[:], float(E - 1), None, ALU.min)
                elif 12 <= k <= 15:
                    ts = slice(TPB * (k - 12), TPB * (k - 12) + TPB)
                    for i in range(2):
                        v.tensor_tensor(oht[:, i, ts, :], tile16[:].unsqueeze(1).to_broadcast([P, TPB, SLOT_TILES]),
                                        tilf[:, i, ts].unsqueeze(2).to_broadcast([P, TPB, SLOT_TILES]), ALU.is_equal)
                    dve.drain()
                    for i in range(2):
                        v.tensor_tensor(oht[:, i, ts, :], oht[:, i, ts, :],
                                        token_id[:, i, ts].unsqueeze(2).to_broadcast([P, TPB, SLOT_TILES]), ALU.mult)
                        ins = v.tensor_tensor(ohl_[:, i, ts, :], lane16[:].unsqueeze(1).to_broadcast([P, TPB, P]),
                                              lanf[:, i, ts].unsqueeze(2).to_broadcast([P, TPB, P]), ALU.is_equal)
                    ins.then_inc(s_oh, 1)
                elif k == 17:
                    dve.wait_ge(s_ixp, cc + 1)
                    scratch = [a[:].rearrange("p t e -> p (t e)")[:, 0:SLOT_TILES] for a in (key, lg2, lg)]
                    code, far, row = scratch
                    v.tensor_copy(code, IX)
                    dve.drain()
                    v.tensor_scalar(far, code, 0.0, float(CHUNK), ALU.is_lt, ALU.mult)
                    v.tensor_scalar(row, code, 0.0, -2.0, ALU.is_lt, ALU.mult)
                    dve.drain()
                    v.scalar_tensor_tensor(out=row, in0=row, scalar=1.0, in1=code, op0=ALU.add, op1=ALU.mult)
                    dve.drain()
                    v.tensor_scalar(row, row, -1.0, None, ALU.add)
                    v.scalar_tensor_tensor(out=code, in0=code, scalar=0.0, in1=pad_row[:],
                                           op0=ALU.is_equal, op1=ALU.mult)
                    dve.drain()
                    v.tensor_scalar(idx[:, cp, :], row, 0.0, None, ALU.max)
                    v.tensor_tensor(far, far, code, ALU.add)
                    dve.drain()
                    v.tensor_tensor(sidx[:, cp, :], row, far, ALU.add).then_inc(s_idx, 1)

            def x_step(cc, s):
                if 0 <= s - 5 < SLOT_TILES:
                    i = tile_of(cc, s - 5)
                    dve.wait_ge(s_y, i + 1)
                    if i - G < tile_of(CHUNKS, 0):
                        wait(dve, s_ys[i % G], 16 * (i // G))
                    else:
                        dve.wait_ge(s_sc[i % G], 16 * scattered(i % G, i))
                    v.tensor_reduce(ysb[:, i % G, :], ybank.rearrange("p (a d) -> p d a", a=2), AX.X, ALU.add).then_inc(s_yc, 1)
                if s < SLOT_TILES:
                    i = tile_of(cc, s)
                    dve.wait_ge(s_xp, i + 1)
                    wait(dve, s_h, i - 2)
                    v.tensor_copy(xT[:, i % 3, :], xbank[i % 2]).then_inc(s_xt, 1)
                if 0 <= s - 3 < SLOT_TILES:
                    i = tile_of(cc, s - 3)
                    dve.wait_ge(s_gh, i + 1)
                    wait(dve, s_y, i - 2)
                    v.tensor_tensor(gl[:, i % 3, :], g32[:, i % 3, :], gh[:, i % 3, :], ALU.subtract).then_inc(s_gl, 1)

            def combine(layer, b, k):
                cp = (CHUNKS * layer + b // BPC) % 2
                if k == 0:
                    dve.wait_ge(s_res, B * layer + b + 1)
                    if layer:
                        dve.wait_ge(s_cl[b % 2], 16 * 2 * (b // 2 + 1))
                    else:
                        dve.wait_ge(s_cg[b % 2], 16 * GATHERS * (b // 2 + 1))
                else:
                    dve.drain()
                for t in range(TPB):
                    tile = xs[:, TPB * b + t, :]
                    at = (b % BPC) * TPB + t
                    ins = v.scalar_tensor_tensor(out=tile, in0=cg[:, b % 2, t, k, :], scalar=wk2[:, cp, k, at:at + 1],
                                                 in1=tile, op0=ALU.mult, op1=ALU.add)
                if k:
                    ins.then_inc(s_cd, 1)

            def front(b, j):
                if j in (0, 1):
                    if b >= BPC:
                        combine(0, b, j)
                elif j == 2:
                    dve.drain()
                    norm_begin(TPB * b, 0, 0)
                elif j == 3:
                    norm_end(z_attn(b), 0, 0)
                    normalise(z_attn(b), TPB * b, 0, 0)
                elif j in (6, 8):
                    i, bias = (0, bq_s) if j == 6 else (1, bk_s)
                    dve.wait_ge(s_hi, 2 * b + i + 1)
                    wait(dve, s_dump, 64 * b)
                    v.scalar_tensor_tensor(out=lo[:, i, :], in0=bank[1][:, :], scalar=bias[:, 0:1], in1=hi[:, i, :],
                                           op0=ALU.add, op1=ALU.subtract).then_inc(s_lo, 1)

            def beside(layer, s):
                for k in range(2):
                    if combined_at(layer, s - k) is not None:
                        combine(layer, combined_at(layer, s - k), k)
                if layer == 0 and prepared_at(s):
                    front(*prepared_at(s))

            first_router(a_step, r_step)
            layer_pass(a_step, r_step, x_step, beside, 0)

            def reduce(b, j):
                s, qt = j // TPB, j % TPB
                w = 256 if qt else 128
                m = mband if qt else mlower
                if j == 0:
                    wait(dve, s_mtp, 2 * b)
                for half in range(2):
                    dve.wait_ge(s_s, 2 * (UNITS * b + j) + half + 1)
                    for g in range(2 * half, 2 * half + 2):
                        src = sbank[:, half, w * (g % 2):w * (g % 2) + w]
                        ins = v.tensor_tensor_reduce(out=src, in0=src, in1=m[:], scale=1.0, scalar=-3e38, op0=ALU.add,
                                                     op1=ALU.max, accum_out=mx[:, qt, 4 * s + g:4 * s + g + 1])
                    ins.then_inc(s_red, 1)

            def back(b):
                for qt in range(TPB):
                    dve.wait_ge(s_ut, TPB * b + qt + 1)
                    u = sbank[:, qt % 2, :].rearrange("p (h r) -> p h r", r=32)
                    v.reciprocal(rden[:, qt, :], u[:, :, DK])
                    dve.drain()
                    v.tensor_tensor(cx[:, qt, :].rearrange("p (h j) -> p h j", j=DK), u[:, :, 0:DK],
                                    rden[:, qt, :].unsqueeze(2).to_broadcast([P, NH, DK]), ALU.mult).then_inc(s_cx, 1)
                dve.wait_ge(s_o, b + 1)
                v.tensor_tensor(flat(b), flat(b), bank[1][:, :], ALU.add).then_inc(s_oa, 1)

            for j in range(UNITS):
                reduce(0, j)
                if j in (MAX_AT, UNITS - 1):
                    front(2, 2 if j == MAX_AT else 3)
            for b in range(B):
                for j in range(UNITS):
                    if b + 1 < B:
                        reduce(b + 1, j)
                    front_in_attention(front, b, j)
                    router_in_attention(r_step, b, j)
                back(b)
            dve.drain()
            layer_pass(a_step, r_step, x_step, beside, 1)
            for b in range(BPC, B):
                for k in range(2):
                    combine(1, b, k)

        @block.scalar
        def _(act):
            a = nc.scalar

            def evac_z(n, affine=False):
                act.wait_ge(s_zp, n + 1)
                wait(act, s_ztf, n - 1)
                src = z_bank(n)
                if affine:
                    a.activation(zT[:, n % 2, :], src[:, :], ACT.Identity, scale=ga_s[:, 0:1],
                                 bias=be_s[:, 0:1]).then_inc(s_zt, 1)
                else:
                    a.activation(zT[:, n % 2, :], src[:, :], ACT.Copy).then_inc(s_zt, 1)

            def a_step(c, k):
                if 0 <= k - 2 < BPC:
                    evac_z(z_linear(BPC * c + k - 2))

            def r_step(cc, k):
                i = k - 3
                if 0 <= i < BPC:
                    act.wait_ge(s_xn, BPC * cc + i + 1)
                    if i >= 2:
                        act.wait_ge(s_tbd[i % 2], 16 * (2 * cc + 1))
                    elif cc:
                        act.wait_ge(s_tbd[i % 2], 16 * 2 * cc)
                    a.activation(tb[:, i % 2, :, 0, :], xnb[:, i % 2], ACT.Copy).then_inc(s_xh, 1)
                i = k - 2
                if 0 <= i < BPC:
                    evac_z(z_router(cc, i), True)
                    for t in range(TPB * i, TPB * i + TPB):
                        tile = xs[:, CT * (cc % CHUNKS) + t, :]
                        ins = a.activation(tile, tile, ACT.Identity, scale=r1p[:, t:t + 1], bias=nmr[:, t:t + 1])
                    ins.then_inc(s_res, 1)
                if k == 8:
                    act.wait_ge(s_lc, cc + 1)
                    a.activation(pr[:], lg[:], ACT.Exp, scale=1.0 / TEMP).then_inc(s_pe, 1)
                if cc == 0 and k in (6, 8):
                    split_high((k - 6) // 2)

            def x_step(cc, s):
                if 0 <= s - 2 < SLOT_TILES:
                    i = tile_of(cc, s - 2)
                    act.wait_ge(s_h, i + 1)
                    wait(act, s_gl, i - 2)
                    wait(act, s_y, i - 2)
                    a.activation(g32[:, i % 3, :], hbank[i % 2], ACT.Silu, scale=1.0 / WSCALE)
                    a.activation(gh[:, i % 3, :], hbank[i % 2], ACT.Silu, scale=1.0 / WSCALE).then_inc(s_gh, 1)

            def beside(layer, s):
                if layer == 0 and prepared_at(s):
                    front(*prepared_at(s))

            def split_high(w):
                act.wait_ge(s_wff[w], 16)
                a.activation(wff[:, :, 2 * w, :], stage[:, w, :].rearrange("p (e n) -> p e n", e=E), ACT.Copy,
                             scale=WSCALE)
                a.activation(stage[:, w, :], stage[:, w, :], ACT.Copy, scale=WSCALE).then_inc(s_wh, 1)

            def front(b, j):
                slot = b % 3
                if j == 5:
                    evac_z(z_attn(b))
                elif j in (6, 8):
                    i, bias = (0, bq_s) if j == 6 else (1, bk_s)
                    act.wait_ge(s_qk, 2 * b + i + 1)
                    wait(act, s_dump, 64 * b)
                    a.activation(hi[:, i, :], bank[1][:, :], ACT.Identity, bias=bias[:, 0:1]).then_inc(s_hi, 1)
                elif j == 10:
                    act.wait_ge(s_vm, b + 1)
                    wait(act, s_pv, UNITS * (b - 2))
                    dst = vp[:, slot, :, 0:NH * VW].rearrange("p t (h j) -> p t h j", j=VW)
                    for t in range(TPB):
                        ins = a.activation(dst[:, t, :, 0:DK], bank[1][:, P * t:P * t + P].rearrange("p (h j) -> p h j", j=DK), ACT.Copy)
                    ins.then_inc(s_v, 1)
                elif j == 12:
                    act.wait_ge(s_vs, 2 * b + 1)
                    a.activation(vrow[:], bank[1][0:1, 0:D], ACT.Copy, scale=ATTN_EPS).then_inc(s_vsr, 1)
                elif j == 13:
                    act.wait_ge(s_vs, 2 * b + 2)
                    a.activation(vsum[:, slot, :], bank[1][:, 0:1], ACT.Copy).then_inc(s_vsr, 1)

            act.wait_ge(s_wcp, 1)
            a.activation(wc[:], bank[0][:, 0:D], ACT.Copy).then_inc(s_wcs, 1)
            a.activation(cb[:], bank[0][0:1, D:2 * D], ACT.Copy).then_inc(s_wcs, 1)
            first_router(a_step, r_step)
            layer_pass(a_step, r_step, x_step, beside, 0)

            def exps(b, j):
                kt = j % TPB
                w = 256 if kt < TPB - 1 else 128
                i = UNITS * b + j
                act.wait_ge(s_st, i + 1)
                wait(act, s_pv, i - 2)
                src = stbank[:].rearrange("p a n -> p (a n)")[:, 1024 * (j % 2):1024 * (j % 2) + 4 * w]
                a.activation(pT[:, i % 3, 0:4 * w], src, ACT.Exp, scale=SCALE).then_inc(s_e, 1)

            def u_copy(b, s):
                act.wait_ge(s_pv, UNITS * b + TPB * (s + 1))
                wait(act, s_ut, TPB * b)
                a.activation(uT[:, s, :], bank[0][:, :], ACT.Copy).then_inc(s_u, 1)

            def ctx_copy(b):
                act.wait_ge(s_cxp, b + 1)
                a.activation(cT, bank[0][:, :], ACT.Identity, bias=vsum[:, b % 3, :]).then_inc(s_ct, 1)

            def max_copy(b, part):
                n = MAX_SPLIT if part == 0 else NH - MAX_SPLIT
                act.wait_ge(s_mtp, 2 * b + part + 1)
                wait(act, s_md, 16 * (2 * b + part))
                a.activation(mT[0:n], bank[1][0:n, :], ACT.Copy, scale=-1.0).then_inc(s_mt, 1)

            max_copy(0, 0)
            exps(0, 0)
            exps(0, 1)
            max_copy(0, 1)
            for b in range(B):
                for j in range(UNITS):
                    if j > 1 and j % TPB == 1:
                        u_copy(b, j // TPB - 1)
                    if j >= 2:
                        exps(b, j)
                    front_in_attention(front, b, j)
                    if j == MAX_AT and b + 1 < B:
                        max_copy(b + 1, 0)
                    router_in_attention(r_step, b, j)
                if b + 1 < B:
                    exps(b + 1, 0)
                u_copy(b, SETS - 1)
                if b + 1 < B:
                    max_copy(b + 1, 1)
                    exps(b + 1, 1)
                ctx_copy(b)
            layer_pass(a_step, r_step, x_step, beside, 1)

        @block.tensor
        def _(pe):
            mm = pe.matmul
            pe.wait_ge(s_const, N_CONST)
            pe.wait_ge(s_wa, 16 * 2)
            mm(bank[0][:, 0:D], wa_s[:], tri[:], start=True, stop=True)
            mm(bank[0][0:1, D:2 * D], ba_s[:], tri[:], start=True, stop=True).then_inc(s_wcp, 1)
            pe.wait_ge(s_wcs, 2)

            def transpose_z(n):
                dst = z_bank(n)
                pe.wait_ge(s_z, n + 1)
                wait(pe, s_zt, n)
                for t in range(TPB):
                    ins = pe.transpose(dst[:, P * t:P * t + P], zr[:, n % 2, t, :], ident[:])
                ins.then_inc(s_zp, 1)

            def a_step(c, k):
                if 0 <= k - 2 < BPC:
                    transpose_z(z_linear(BPC * c + k - 2))
                if 0 <= k - 3 < BPC:
                    b = BPC * c + k - 3
                    n = z_linear(b)
                    pe.wait_ge(s_zt, n + 1)
                    wait(pe, s_aa, b)
                    if c and k == 3:
                        pe.wait_ge(s_idx, 1)
                    for t in range(TPB):
                        o = bank[1][:, P * t:P * t + P]
                        mm(o, zT[:, n % 2, P * t:P * t + P], wc[:], start=True, stop=False)
                        ins = mm(o, ones_row[:], cb[:], start=False, stop=True)
                    ins.then_inc(s_am, 1)
                    pe.sem_inc(s_ztf, 1)

            def r_step(cc, k):
                ohl_ = cg[:].rearrange("p s t k d -> p (s t k d)").bitcast(F16).rearrange(
                    "p (k t n) -> p k t n", k=2, t=CT) if cc == CHUNKS else ohl
                if 0 <= k - 2 < BPC:
                    if cc == 0 and k == 2:
                        pe.wait_ge(s_w, 16 * N_W)
                    if cc == CHUNKS and k == 2:
                        pe.wait_ge(s_cx, TPB * (B - 1))
                    transpose_z(z_router(cc, k - 2))
                if 0 <= k - 3 < BPC:
                    i = k - 3
                    n = z_router(cc, i)
                    pe.wait_ge(s_zt, n + 1)
                    if i == 0:
                        wait(pe, s_lc, cc)
                    for t in range(TPB):
                        ins = mm(logits_bank(cc)[:, TPB * i + t, :], zT[:, n % 2, P * t:P * t + P], rw_s[:], start=True, stop=True)
                    if i == BPC - 1:
                        ins.then_inc(s_lg, 1)
                    pe.sem_inc(s_ztf, 1)
                if k == 9:
                    pe.wait_ge(s_aa, BPC * min(cc + 1, CHUNKS))
                    wait(pe, s_idx, cc)
                    wait(pe, s_oa, (B - 1) * (cc // CHUNKS))
                    pe.wait_ge(s_c16, cc + 1)
                    mm(RK, before16[:], c16[:], start=True, stop=False, skip_group_check=True)
                    for t in range(CT - 1):
                        n = CT - 1 - t
                        mm(RK[:, t + 1:CT, :], ones16[:], c16[:, t:t + 1, :].to_broadcast([P, n, E]), start=False,
                           stop=(t == CT - 2), skip_group_check=True)
                    for t in range(CT):
                        ins = mm(CN, ones16[:], c16[:, t, :], start=(t == 0), stop=(t == CT - 1))
                    ins.then_inc(s_cn, 1)
                elif 13 <= k <= 16:
                    pe.wait_ge(s_oh, 4 * cc + k - 12)
                    for t in range(TPB * (k - 13), TPB * (k - 13) + TPB):
                        for i in range(2):
                            ins = mm(IX, ohl_[:, i, t, :], oht[:, i, t, :], start=(t == 0 and i == 0),
                                     stop=(t == CT - 1 and i == 1))
                    if k == 16:
                        ins.then_inc(s_ixp, 1)

            def x_step(cc, s):
                if s == 0:
                    pe.wait_ge(s_wl, 2)
                    pe.wait_ge(s_idx, cc + 1)
                if s < SLOT_TILES:
                    i = tile_of(cc, s)
                    pe.wait_ge(s_g[i % G], 16 * (i // G + 1))
                    wait(pe, s_xt, i - 1)
                    for a2 in range(2):
                        ins = pe.transpose(xbank[i % 2][:, P * a2:P * a2 + P], xg[:, i % G, a2, :], ident16[:])
                    ins.then_inc(s_xp, 1)
                if s % LOADS == 0 and s < SLOT_TILES:
                    n = min(LOADS, SLOT_TILES - s)
                    _, ids = nc.values_load_multi_w_load_instructions(
                        eid[0:1, cc % 2, s:s + n], [mybir.EngineType.PE], min_val=0, max_val=E - 1,
                        skip_runtime_bounds_check_because="a count of thresholds passed, cut off at E - 1")
                    for k in range(n):
                        experts[s + k] = wff[:, bass.ds(ids[k], 1), :, :]
                if 0 <= s - 2 < SLOT_TILES:
                    i = tile_of(cc, s - 2)
                    pe.wait_ge(s_xt, i + 1)
                    wait(pe, s_gh, i - 1)
                    xh, xl = xT[:, i % 3, 0:P], xT[:, i % 3, P:2 * P]
                    w = experts[s - 2]
                    for f in range(FC):
                        o = hbank[i % 2][:, P * f:P * f + P]
                        wh, wl = w[:, 0, 0, P * f:P * f + P], w[:, 0, 1, P * f:P * f + P]
                        mm(o, wh, xh, start=True, stop=False)
                        mm(o, wh, xl, start=False, stop=False)
                        ins = mm(o, wl, xh, start=False, stop=True)
                    ins.then_inc(s_h, 1)
                if 0 <= s - 4 < SLOT_TILES:
                    i = tile_of(cc, s - 4)
                    pe.wait_ge(s_gl, i + 1)
                    wait(pe, s_yc, i)
                    o = ybank
                    w = experts[s - 4]
                    for f in range(FC):
                        whl = w[:, 0, 2:4, P * f:P * f + P]
                        mm(o, gh[:, i % 3, P * f:P * f + P], whl, start=(f == 0), stop=False, skip_group_check=True)
                        ins = mm(o[:, 0:P], gl[:, i % 3, P * f:P * f + P], whl[:, 0, :], start=False, stop=(f == FC - 1),
                                 skip_group_check=True)
                    ins.then_inc(s_y, 1)

            experts = {}

            def beside(layer, s):
                if layer == 0 and prepared_at(s):
                    front(*prepared_at(s))

            def front(b, j):
                n = z_attn(b)
                slot = b % 3
                if j == 5:
                    wait(pe, s_oa, b - 2)
                    wait(pe, s_vsr, 2 * b)
                    wait(pe, s_mt, 2 * (b - 1))
                    transpose_z(n)
                elif j == 6:
                    pe.wait_ge(s_zt, n + 1)
                    mm(bank[1][:, :], wq_s[:], zT[:, n % 2, :], start=True, stop=True).then_inc(s_qk, 1)
                elif j == 8:
                    pe.wait_ge(s_lo, 2 * b + 1)
                    mm(bank[1][:, :], wk_s[:], zT[:, n % 2, :], start=True, stop=True).then_inc(s_qk, 1)
                elif j == 10:
                    pe.wait_ge(s_lo, 2 * b + 2)
                    for t in range(TPB):
                        o = bank[1][:, P * t:P * t + P]
                        mm(o, zT[:, n % 2, P * t:P * t + P], wv_s[:], start=True, stop=False)
                        ins = mm(o, ones_row[:], bv_s[:], start=False, stop=True)
                    ins.then_inc(s_vm, 1)
                    pe.sem_inc(s_ztf, 1)
                elif j == 12:
                    pe.wait_ge(s_v, b + 1)
                    for t in range(TPB):
                        vt = vp[:, slot, t, 0:NH * VW].rearrange("p (h j) -> p h j", j=VW)[:, :, 0:DK]
                        ins = mm(bank[1][0:1, 0:D], ones_col[:], vt, start=(t == 0), stop=(t == TPB - 1))
                    ins.then_inc(s_vs, 1)
                elif j == 13:
                    pe.wait_ge(s_vsr, 2 * b + 1)
                    mm(bank[1][:, 0:1], vrow[:], ones_row[0:1, 0:1], start=True, stop=True).then_inc(s_vs, 1)

            first_router(a_step, r_step)
            layer_pass(a_step, r_step, x_step, beside, 0)
            pe.wait_ge(s_yc, tile_of(CHUNKS, 0))

            def scores(b, j, half):
                s, qt = j // TPB, j % TPB
                slot = b % 3
                if j == 0 and half == 0:
                    pe.wait_ge(s_stk[b % 2], 16 * 24 * (b // 2 + 1))
                    wait(pe, s_cx, TPB * (b - 1))
                wait(pe, s_red, 2 * (UNITS * b + j) + half - 1)
                w = 256 if qt else 128
                k0 = P * (qt - 1) if qt else 0
                for g in range(2 * half, 2 * half + 2):
                    ins = mm(sbank[:, half, w * (g % 2):w * (g % 2) + w], qz[0:P - 1, slot, 4 * s + g, P * qt:P * qt + P],
                             kst[0:P - 1, slot, s, k0:k0 + w], start=True, stop=True)
                ins.then_inc(s_s, 1)

            def scores_t(b, j):
                s, kt = j // TPB, j % TPB
                slot = b % 3
                if j in (0, MAX_SPLIT):
                    pe.wait_ge(s_mr[int(j > 0)], 16 * (b + 1))
                wait(pe, s_e, UNITS * b + j - 1)
                w = 256 if kt < TPB - 1 else 128
                bank_ = stbank[:].rearrange("p a n -> p (a n)")[:, 1024 * (j % 2):1024 * (j % 2) + 1024]
                for g in range(4):
                    ins = mm(bank_[:, w * g:w * g + w], kst[:, slot, s, P * kt:P * kt + P],
                             qz[:, slot, 4 * s + g, P * kt:P * kt + w], start=True, stop=True)
                ins.then_inc(s_st, 1)

            def pv(b, j):
                s, kt = j // TPB, j % TPB
                w = 256 if kt < TPB - 1 else 128
                i = UNITS * b + j
                pe.wait_ge(s_pm, i + 1)
                if kt == 0:
                    wait(pe, s_u, SETS * b + s)
                    if s == 0:
                        wait(pe, s_ct, b)
                for g in range(4):
                    h = SETS * s + g
                    ins = mm(bank[0][32 * g:32 * g + 32, P * kt:P * kt + w], vp[:, b % 3, kt, VW * h:VW * h + 32],
                             pT[:, i % 3, w * g:w * g + w], start=(kt == 0), stop=(kt == TPB - 1),
                             tile_position=(0, 32 * g), skip_group_check=True)
                ins.then_inc(s_pv, 1)

            def max_rows(b, part):
                cols = slice(0, MAX_SPLIT) if part == 0 else slice(MAX_SPLIT, NH)
                if part == 0:
                    pe.wait_ge(s_red, 2 * (UNITS * b + MAX_SPLIT))
                    pe.wait_ge(s_vsr, 2 * min(b + 2, B))
                    wait(pe, s_oa, b - 1)
                else:
                    pe.wait_ge(s_red, 2 * UNITS * (b + 1))
                    pe.wait_ge(s_mt, 2 * b + 1)
                for t in range(TPB):
                    ins = pe.transpose(bank[1][0:cols.stop - cols.start, P * t:P * t + P], mx[:, t, cols], ident[:])
                ins.then_inc(s_mtp, 1)

            def back(b):
                pe.wait_ge(s_u, SETS * (b + 1))
                for qt in range(TPB):
                    if qt >= 2:
                        pe.wait_ge(s_cx, TPB * b + qt - 1)
                    for s in range(SETS):
                        ins = pe.transpose(sbank[:, qt % 2, P * s:P * s + P], uT[:, s, P * qt:P * qt + P], ident[:])
                    ins.then_inc(s_ut, 1)
                for qt in range(TPB):
                    pe.wait_ge(s_cx, TPB * b + qt + 1)
                    ins = pe.transpose(bank[0][:, P * qt:P * qt + P], cx[:, qt, :], ident[:])
                ins.then_inc(s_cxp, 1)
                pe.wait_ge(s_ct, b + 1)
                pe.wait_ge(s_mt, 2 * min(b + 2, B))
                for t in range(TPB):
                    o = bank[1][:, P * t:P * t + P]
                    mm(o, cT[:, P * t:P * t + P], wo_s[:], start=True, stop=False)
                    ins = mm(o, ones_row[:], bo_s[:], start=False, stop=True)
                ins.then_inc(s_o, 1)

            for j in range(UNITS):
                scores(0, j, 0)
                scores(0, j, 1)
                if j == MAX_AT:
                    max_rows(0, 0)
            scores_t(0, 0)
            scores_t(0, 1)
            max_rows(0, 1)
            for b in range(B):
                for j in range(UNITS + 2):
                    if j >= 2:
                        pv(b, j - 2)
                    if j < UNITS:
                        if b + 1 < B:
                            scores(b + 1, j, 0)
                        if j >= 2:
                            scores_t(b, j)
                        front_in_attention(front, b, j)
                        if b + 1 < B:
                            scores(b + 1, j, 1)
                            if j == MAX_AT:
                                max_rows(b + 1, 0)
                        router_in_attention(r_step, b, j)
                    elif b + 1 < B:
                        scores_t(b + 1, j - UNITS)
                if b + 1 < B:
                    max_rows(b + 1, 1)
                else:
                    pe.wait_ge(s_idx, CHUNKS + 1)
                back(b)
            pe.wait_ge(s_oa, B)
            layer_pass(a_step, r_step, x_step, beside, 1)


def head_order():
    return [DK * (SETS * s + g) + j for g in range(4) for s in range(SETS) for j in range(DK)]


def kernel(L0_attn_a_x, L0_attn_a_W, L0_attn_a_bias, L0_attn_b_Wq, L0_attn_b_bq, L0_attn_b_Wk, L0_attn_b_bk,
           L0_attn_b_Wv, L0_attn_b_bv, L0_attn_b_Wo, L0_attn_b_bo, L0_ffn_gamma, L0_ffn_beta, L0_ffn_router_w,
           L0_ffn_W1, L0_ffn_W2):
    import numpy as np
    import concourse.bacc as bacc
    from concourse.bass_utils import run_bass_kernel_spmd

    order = head_order()
    layout = {
        "x": L0_attn_a_x, "wa": L0_attn_a_W, "ba": np.reshape(L0_attn_a_bias, (D, 1)),
        "wq": np.transpose(L0_attn_b_Wq)[:, order], "wk": np.transpose(L0_attn_b_Wk)[:, order],
        "wv": np.transpose(L0_attn_b_Wv), "wo": np.transpose(L0_attn_b_Wo),
        "bq": np.reshape(np.asarray(L0_attn_b_bq)[order], (D, 1)), "bk": np.reshape(np.asarray(L0_attn_b_bk)[order], (D, 1)),
        "bv": np.reshape(L0_attn_b_bv, (1, D)), "bo": np.reshape(L0_attn_b_bo, (1, D)),
        "gamma": np.reshape(L0_ffn_gamma, (D, 1)), "beta": np.reshape(L0_ffn_beta, (D, 1)),
        "rw": np.transpose(L0_ffn_router_w), "w1": L0_ffn_W1, "w2": L0_ffn_W2,
    }
    nc = bacc.Bacc("TRN2", target_bir_lowering=False, num_devices=1)
    arrays, args = {}, []
    for name, a in layout.items():
        a = np.ascontiguousarray(a)
        arrays[f"in_{name}"] = a
        args.append(nc.dram_tensor(f"in_{name}", a.shape, mybir.dt.from_np(a.dtype), kind="ExternalInput").ap())
    args.append(nc.dram_tensor("out", (B, SEQ, D), F32, kind="ExternalOutput").ap())
    build(nc, *args)
    r = run_bass_kernel_spmd(nc, [arrays], core_ids=[0])
    return r.results[0]["out"]
```
